# Optimizing a Trainium2 kernel written in Bass

```python
import numpy as np
import jax
import jax.numpy as jnp

def _softmax(x, axis=-1):
    return jax.nn.softmax(x, axis=axis)

def _gelu(x):
    return jax.nn.gelu(x, approximate=True)

def _silu(x):
    return jax.nn.silu(x)

def _sigmoid(x):
    return jax.nn.sigmoid(x)

def _layernorm(x, axis=-1, eps=1e-05):
    m = jnp.mean(x, axis=axis, keepdims=True)
    v = jnp.var(x, axis=axis, keepdims=True)
    return (x - m) / jnp.sqrt(v + eps)

def _scatter_add(tgt, idx, src, axis=0):
    return tgt.at[idx].add(src)

def _segment_sum(src, seg, n):
    return jax.ops.segment_sum(src, seg, n)
kernel_name = 'mk_xattn_seq_d2_seqx_r2_ca45b9'

def setup_inputs(seed: int=0):
    np.random.seed(seed)
    _w = jnp.asarray

    def _rec_inputs():
        import jax
        import jax.numpy as jnp
        _rk = jax.random.key(seed)
        x = 7.22e-05 + 1 * jax.random.normal(jax.random.fold_in(_rk, 1), (8, 512, 512), jnp.float32)
        _lenS = 512 - jax.random.randint(jax.random.fold_in(_rk, 7), (8,), 0, max(1, 512 // 4) + 1, jnp.int32)
        _lenS2 = 512 - jax.random.randint(jax.random.fold_in(_rk, 8), (8,), 0, max(1, 512 // 4) + 1, jnp.int32)
        _ctx_1024P = jax.random.normal(jax.random.fold_in(_rk, 11), (8, 16, 512), jnp.float32)
        _ctx_1024c = jax.random.dirichlet(jax.random.fold_in(_rk, 511), 0.3 * jnp.ones((16,), jnp.float32), (8, 512))
        _ctx_1024t = jnp.einsum('bsk,bkd->bsd', _ctx_1024c, _ctx_1024P)
        _ctx_1024t = _ctx_1024t * jax.lax.rsqrt(jnp.mean(jnp.square(_ctx_1024t)) + 1e-12) * 0.953939
        ctx_1024 = 4.13588e-05 + 0.999923 * (_ctx_1024t + 0.3 * jax.random.normal(jax.random.fold_in(_rk, 611), (8, 512, 512), jnp.float32))
        return (x, ctx_1024)
    x, ctx_1024 = _rec_inputs()

    def _L0_xattn_setup():
        import jax, jax.numpy as jnp
        import numpy as np
        NH = 16
        key = jax.random.key(seed)
        ks = jax.random.split(key, 5)
        B, N, D = (4, 1024, 512)
        return {'tgt': jax.random.normal(ks[0], (B, N, D), dtype=jnp.float32), 'memory': jax.random.normal(ks[1], (B, N, D), dtype=jnp.float32), 'Wq': jax.random.normal(ks[2], (D, D), dtype=jnp.float32) * (1.0 / np.sqrt(D)), 'Wk': jax.random.normal(ks[3], (D, D), dtype=jnp.float32) * (1.0 / np.sqrt(D)), 'Wv': jax.random.normal(ks[4], (D, D), dtype=jnp.float32) * (1.0 / np.sqrt(D))}
    _L0_xattn_all = _L0_xattn_setup()
    _L0_xattn_in = {k: v for k, v in _L0_xattn_all.items() if k in ('Wq', 'Wk', 'Wv')}
    del _L0_xattn_all

    def _L1_xattn_setup():
        import jax, jax.numpy as jnp
        import numpy as np
        DIM = 512
        HEADS = 16
        HEAD_DIM = DIM // HEADS
        HIDDEN = int(DIM * 4.0)
        SCALE = HEAD_DIM ** (-0.5)
        EPS = 1e-05

        def layer_norm(x, g, b):
            mu = jnp.mean(x, axis=-1, keepdims=True)
            var = jnp.var(x, axis=-1, keepdims=True)
            return (x - mu) * jax.lax.rsqrt(var + EPS) * g + b
        key = jax.random.key(seed)
        ks = jax.random.split(key, 16)
        s = 0.02
        return {'x': jax.random.normal(ks[0], (4, 512, DIM), dtype=jnp.float32), 'y': jax.random.normal(ks[1], (4, 1024, DIM), dtype=jnp.float32), 'gq': jnp.ones((DIM,), jnp.float32), 'bq': jnp.zeros((DIM,), jnp.float32), 'gkv': jnp.ones((DIM,), jnp.float32), 'bkv': jnp.zeros((DIM,), jnp.float32), 'Wq': jax.random.normal(ks[2], (DIM, DIM), jnp.float32) * s, 'Wkv': jax.random.normal(ks[3], (DIM, 2 * DIM), jnp.float32) * s, 'Wproj': jax.random.normal(ks[4], (DIM, DIM), jnp.float32) * s, 'bproj': jnp.zeros((DIM,), jnp.float32), 'gm': jnp.ones((DIM,), jnp.float32), 'bm': jnp.zeros((DIM,), jnp.float32), 'W1': jax.random.normal(ks[5], (DIM, HIDDEN), jnp.float32) * s, 'b1': jnp.zeros((HIDDEN,), jnp.float32), 'W2': jax.random.normal(ks[6], (HIDDEN, DIM), jnp.float32) * s, 'b2': jnp.zeros((DIM,), jnp.float32)}
    _L1_xattn_all = _L1_xattn_setup()
    _L1_xattn_in = {k: v for k, v in _L1_xattn_all.items() if k in ('gq', 'bq', 'gkv', 'bkv', 'Wq', 'Wkv', 'Wproj', 'bproj', 'gm', 'bm', 'W1', 'b1', 'W2', 'b2')}
    del _L1_xattn_all
    return {'x': x, 'ctx_1024': ctx_1024, 'L0_xattn_Wq': _L0_xattn_in['Wq'], 'L0_xattn_Wk': _L0_xattn_in['Wk'], 'L0_xattn_Wv': _L0_xattn_in['Wv'], 'L1_xattn_gq': _L1_xattn_in['gq'], 'L1_xattn_bq': _L1_xattn_in['bq'], 'L1_xattn_gkv': _L1_xattn_in['gkv'], 'L1_xattn_bkv': _L1_xattn_in['bkv'], 'L1_xattn_Wq': _L1_xattn_in['Wq'], 'L1_xattn_Wkv': _L1_xattn_in['Wkv'], 'L1_xattn_Wproj': _L1_xattn_in['Wproj'], 'L1_xattn_bproj': _L1_xattn_in['bproj'], 'L1_xattn_gm': _L1_xattn_in['gm'], 'L1_xattn_bm': _L1_xattn_in['bm'], 'L1_xattn_W1': _L1_xattn_in['W1'], 'L1_xattn_b1': _L1_xattn_in['b1'], 'L1_xattn_W2': _L1_xattn_in['W2'], 'L1_xattn_b2': _L1_xattn_in['b2']}

def reference(x, ctx_1024, L0_xattn_Wq, L0_xattn_Wk, L0_xattn_Wv, L1_xattn_gq, L1_xattn_bq, L1_xattn_gkv, L1_xattn_bkv, L1_xattn_Wq, L1_xattn_Wkv, L1_xattn_Wproj, L1_xattn_bproj, L1_xattn_gm, L1_xattn_bm, L1_xattn_W1, L1_xattn_b1, L1_xattn_W2, L1_xattn_b2):
    import jax
    import jax.numpy as jnp

    def _L0_xattn_ref(tgt, memory, Wq, Wk, Wv):
        import jax, jax.numpy as jnp
        import numpy as np
        NH = 16
        B, N, D = tgt.shape
        dk = D // NH
        scale = 1.0 / np.sqrt(dk)
        q = (tgt @ Wq.T).reshape(B, N, NH, dk).transpose(0, 2, 1, 3)
        k = (memory @ Wk.T).reshape(B, N, NH, dk).transpose(0, 2, 1, 3)
        v = (memory @ Wv.T).reshape(B, N, NH, dk).transpose(0, 2, 1, 3)
        scores = jnp.einsum('bhqd,bhkd->bhqk', q, k) * scale
        probs = jax.nn.softmax(scores, axis=-1)
        att = jnp.einsum('bhqk,bhkd->bhqd', probs, v)
        att = att.transpose(0, 2, 1, 3).reshape(B, N, D)
        tgt2 = att[0]
        return tgt + tgt2

    def _L1_xattn_ref(x, y, gq, bq, gkv, bkv, Wq, Wkv, Wproj, bproj, gm, bm, W1, b1, W2, b2):
        import jax, jax.numpy as jnp
        import numpy as np
        DIM = 512
        HEADS = 16
        HEAD_DIM = DIM // HEADS
        HIDDEN = int(DIM * 4.0)
        SCALE = HEAD_DIM ** (-0.5)
        EPS = 1e-05

        def layer_norm(x, g, b):
            mu = jnp.mean(x, axis=-1, keepdims=True)
            var = jnp.var(x, axis=-1, keepdims=True)
            return (x - mu) * jax.lax.rsqrt(var + EPS) * g + b
        B, M, C = x.shape
        N = y.shape[1]
        xq = layer_norm(x, gq, bq)
        ykv = layer_norm(y, gkv, bkv)
        q = (xq @ Wq).reshape(B, M, HEADS, HEAD_DIM).transpose(0, 2, 1, 3)
        kv = (ykv @ Wkv).reshape(B, N, 2, HEADS, HEAD_DIM).transpose(2, 0, 3, 1, 4)
        k, v = (kv[0], kv[1])
        attn = jax.nn.softmax(jnp.einsum('bhmd,bhnd->bhmn', q, k) * SCALE, axis=-1)
        o = jnp.einsum('bhmn,bhnd->bhmd', attn, v).transpose(0, 2, 1, 3).reshape(B, M, C)
        x = x + o @ Wproj + bproj
        h = layer_norm(x, gm, bm)
        h = jax.nn.gelu(h @ W1 + b1, approximate=False)
        x = x + h @ W2 + b2
        return x
    x = _L0_xattn_ref(x, ctx_1024, L0_xattn_Wq, L0_xattn_Wk, L0_xattn_Wv)
    x = _L1_xattn_ref(x, ctx_1024, L1_xattn_gq, L1_xattn_bq, L1_xattn_gkv, L1_xattn_bkv, L1_xattn_Wq, L1_xattn_Wkv, L1_xattn_Wproj, L1_xattn_bproj, L1_xattn_gm, L1_xattn_bm, L1_xattn_W1, L1_xattn_b1, L1_xattn_W2, L1_xattn_b2)
    return x

_drawn_inputs = setup_inputs


def setup_inputs(seed=0):
    import zlib

    import numpy as np

    out = dict(_drawn_inputs(seed))
    spreads = {'L1_xattn_gq': (1.0, 0.6),
     'L1_xattn_bq': (0.0, 0.8),
     'L1_xattn_gkv': (1.0, 0.6),
     'L1_xattn_bkv': (0.0, 0.463),
     'L1_xattn_bproj': (0.0, 0.1),
     'L1_xattn_gm': (1.0, 0.2),
     'L1_xattn_bm': (0.0, 0.371),
     'L1_xattn_b1': (0.0, 0.1),
     'L1_xattn_b2': (0.0, 0.1)}
    factors = {'L1_xattn_Wq': 8.0}
    for name, (base, spread) in spreads.items():
        noise = np.random.default_rng([zlib.crc32(name.encode()), seed]).standard_normal(out[name].shape)
        drawn = base * np.exp(spread * noise) if base else spread * noise
        out[name] = jnp.asarray(drawn.astype(out[name].dtype))
    for name, factor in factors.items():
        out[name] = (out[name] * factor).astype(out[name].dtype)
    return out
```

```python
import numpy as np

import concourse.bass as bass
from concourse import mybir

F32 = mybir.dt.float32
F32R = mybir.dt.float32r
ACT = mybir.ActivationFunctionType
ALU = mybir.AluOpType
AX = mybir.AxisListType

P = 128
T = 512
D = 512
F = 2048
B = 8
NH = 16
DK = D // NH
FC = D // P
TC = T // P
HC = F // P
G = P // DK
SCALE = float(DK) ** -0.5
EPS = 1e-5

KQ = 3 * DK
KM = KQ + 1
VW = 2 * DK + 1
STEPS = NH + 2
CH = NH * TC
STACK_DMAS = 6
PLACE_DMAS = 3
NCOLS = 6 * FC + HC

PRE_UNITS = 14
PASS_UNITS = 24
PRE_SPLITS = 14
PASS_SPLITS = 20
LAST_UNITS = 14
LAST_SPLITS = 10
TILE_UNITS = HC + FC


class Pass:

    def __init__(self, n, first=False, last=False):
        self.n, self.first, self.last = n, first, last
        units = {}
        splits = {}
        order = [("q", 1), ("k", 1), ("q", 2), ("k", 2), ("q", 3), ("k", 3)]
        if last:
            order += [("h", c) for c in range(FC)] + [("out", c) for c in range(TC)]
        elif first:
            order += [("y", c) for c in range(FC)] + [("k", G)] + [("v", c) for c in range(TC)]
            order += [("out", c) for c in range(TC)] + [("x", c) for c in range(FC)] + [("q", G)]
        else:
            order += [("y", c) for c in range(FC)] + [("k", G)] + [("x", c) for c in range(FC)]
            order += [("q", G)] + [("v", c) for c in range(TC)] + [("out", c) for c in range(TC)]
        for key in order:
            units[key] = len(units)
            if key[0] != "out":
                splits[key] = len(splits)
        self.units, self.splits = units, splits

    def unit(self, kind, c):
        return self.n * PASS_UNITS + (PRE_UNITS + self.units[kind, c])

    def split(self, kind, c):
        return self.n * PASS_SPLITS + (PRE_SPLITS + self.splits[kind, c])

    def bank(self, kind, c):
        return self.units[kind, c] % 2

    def chunk(self, h, c):
        return self.n * CH + (h * TC + c)

    def head(self, h):
        return self.n * NH + h


class Before:

    first, last = True, False

    def __init__(self):
        order = [("y", c) for c in range(FC)] + [("v", c) for c in range(TC)] + [("k", 0)]
        order += [("x", c) for c in range(FC)] + [("q", 0)]
        self.units = {key: n for n, key in enumerate(order)}

    def unit(self, kind, c):
        return self.units[kind, c]

    split = unit

    def bank(self, kind, c):
        return self.units[kind, c] % 2


def xattn_program(nc, x, ctx, l0wq, l0wk, l0wv, wq, wk, wv, wo, w1, w2, cols, bproj, b2, ident, out):
    x2 = nc.dram_tensor("x2_scratch", (B, T, D), F32, kind="Internal").ap()

    place = [-(-nc.sbuf_base // 64) * 64]

    def sb(name, shape, dt, at=None):
        size = 4 * int(np.prod(shape[1:]))
        if at is None:
            at = place[0]
            place[0] += -(-size // 64) * 64
        return nc.alloc_sbuf_tensor_at(name, shape, dt, offset=at)

    weights_at = place[0]
    wq_s = sb("wq_s", [P, 2, FC, D], F32R)
    wk_s = sb("wk_s", [P, 2, FC, D], F32R)
    wv_s = sb("wv_s", [P, 2, FC, D], F32R)
    wo_s = sb("wo_s", [P, 2, FC, D], F32R)
    w2_at = place[0]
    yT = sb("yT", [P, 2, FC, T], F32R)
    q_hl = sb("q_hl", [P, 2, T], F32R)
    k_hl = sb("k_hl", [P, 2, T], F32R)
    q_st = sb("q_st", [P, G, T], F32R)
    k_st = sb("k_st", [P, G, T], F32R)
    v_s = sb("v_s", [P, TC, NH, VW], F32R)
    oT = sb("oT", [P, 2, FC, T], F32R)
    xT = sb("xT", [P, 2, FC, T], F32R)
    p_hi = sb("p_hi", [P, TC, T], F32R)
    p_lo = sb("p_lo", [P, TC, T], F32R)
    tgt2 = sb("tgt2", [P, TC, D], F32)
    xres = sb("xres", [P, TC, D], F32)
    yt = sb("yt", [P, TC, D], F32)
    scr_at = place[0]
    o_a = sb("o_a", [P, T], F32)
    o_b = sb("o_b", [P, T], F32)
    rs = sb("rs", [P, T], F32)
    rs_t = sb("rs_t", [P, T], F32)
    scr = sb("scr", [P, TC, D], F32, at=scr_at)
    o_raw = sb("o_raw", [P, 2, T], F32)
    bp_s = sb("bp_s", [P, D], F32)
    b2_s = sb("b2_s", [P, D], F32)
    id_s = sb("id_s", [P, P], F32)
    id_r = sb("id_r", [P, P], F32R)
    col_s = sb("col_s", [P, NCOLS], F32)
    negmax = sb("negmax", [P, 2, TC], F32R)
    rinv = sb("rinv", [P, T // DK], F32)
    stats = sb("stats", [P, TC, 6], F32)
    mv = sb("mv", [P, TC, 2], F32)
    var_e = sb("var_e", [P, TC], F32)
    rstd = sb("rstd", [P, TC], F32)
    m_half = sb("m_half", [P, TC], F32)
    eps_s = sb("eps_s", [P, TC], F32)
    assert place[0] <= nc.sbuf_usable_end, (place[0], nc.sbuf_usable_end)
    w1_hi = sb("w1_hi", [P, FC, FC, D], F32R, at=weights_at)
    w1_lo = sb("w1_lo", [P, FC, FC, D], F32R, at=weights_at + 4 * FC * FC * D)
    w2_hi = sb("w2_hi", [P, HC, D], F32R, at=w2_at)
    w2_lo = sb("w2_lo", [P, HC, D], F32R, at=w2_at + 4 * HC * D)

    def col(k, c):
        return col_s[:, FC * k + c:FC * k + c + 1]

    GQ, BQ, GKV, BKV, GM, BM = range(6)

    ps_s = nc.alloc_psum_tensor("ps_s", [P, 2, T], F32)
    ps_t = nc.alloc_psum_tensor("ps_t", [P, 2, T], F32)
    ps_o = nc.alloc_psum_tensor("ps_o", [P, T], F32)
    ps_m = nc.alloc_psum_tensor("ps_m", [P, T], F32)
    ps_d = nc.alloc_psum_tensor("ps_d", [P, 2, T], F32)
    out_banks = [ps_s[:, 0], ps_s[:, 1], ps_t[:, 0], ps_t[:, 1]]

    sem = nc.alloc_semaphore
    y_loaded = sem("y_loaded")
    x_loaded = sem("x_loaded")
    res_loaded = sem("res_loaded")
    raw_loaded = {k: sem(f"raw_{k}_loaded") for k in ("yt", "xres", "tgt2", "scr")}
    const_loaded = sem("const_loaded")
    w_hi = sem("w_hi")
    w_split = sem("w_split")
    unit_ready = sem("unit_ready")
    hi_ready = sem("hi_ready")
    split = {k: sem(f"{k}_split") for k in "xyqkvhg"}
    out_done = sem("out_done")
    x_summed = sem("x_summed")
    res_summed = sem("res_summed")
    ln_var = sem("ln_var")
    ln_eps = sem("ln_eps")
    ln_rstd = sem("ln_rstd")
    normed = sem("normed")
    stack_loaded = [sem(f"stack_loaded_{j}") for j in range(G)]
    s_ready = sem("s_ready")
    s_maxed = sem("s_maxed")
    m_spread = sem("m_spread")
    m_moved = sem("m_moved")
    t_ready = sem("t_ready")
    p_exp = sem("p_exp")
    p_split = sem("p_split")
    pv_done = sem("pv_done")
    o_moved = sem("o_moved")
    o_placed = [sem(f"o_placed_{j}") for j in range(G)]
    inv_own = sem("inv_own")
    inv_copied = sem("inv_copied")
    res_own = sem("res_own")
    half_set = sem("half_set")
    inv_ready = sem("inv_ready")
    join_own = sem("join_own")
    o_joined = sem("o_joined")
    consts_set = sem("consts_set")
    ident_set = sem("ident_set")
    stored = sem("stored")
    out_stored = sem("out_stored")
    y2_done = sem("y2_done")

    def rows(dram, b):
        if isinstance(b, int):
            return dram[b].rearrange("(c p) d -> p c d", p=P)
        return dram[bass.ds(b, 1)].rearrange("a (c p) d -> p (a c) d", p=P)

    first, last = Pass(0, first=True), Pass(B, last=True)
    END_UNITS = PRE_UNITS + PASS_UNITS * B + LAST_UNITS
    END_SPLITS = PRE_SPLITS + PASS_SPLITS * B + LAST_SPLITS
    pieces = ["l0wk", "l0wv", "l0wq", "wv", "wo", "wq", "wk", "w1_0", "w1_1"]
    pieces += ["w2_0", "w1_2", "w2_1", "w1_3", "w2_2", "w2_3"]
    piece_no = {name: n for n, name in enumerate(pieces)}
    raw_in = {"l0wk": ("tgt2", 1), "l0wv": ("xres", 1), "l0wq": ("scr", 1), "wv": ("xres", 2),
              "wo": ("xres", 3), "wq": ("yt", 1), "wk": ("tgt2", 2), "w1_0": ("tgt2", 3),
              "w1_1": ("tgt2", 4), "w2_0": ("scr", 2), "w1_2": ("tgt2", 5), "w2_1": ("scr", 3),
              "w1_3": ("tgt2", 6), "w2_2": ("scr", 4), "w2_3": ("tgt2", 7)}
    raw_buf = {"tgt2": tgt2, "xres": xres, "scr": scr, "yt": yt}
    parts = {"l0wk": wk_s, "l0wv": wv_s, "l0wq": wq_s, "wv": wv_s, "wo": wo_s, "wq": wq_s, "wk": wk_s}
    raw_dram = {"l0wk": l0wk, "l0wv": l0wv, "l0wq": l0wq, "wv": wv, "wo": wo, "wq": wq, "wk": wk}
    for j in range(FC):
        raw_dram[f"w1_{j}"] = w1[j]
        raw_dram[f"w2_{j}"] = w2[:, FC * j:FC * j + FC]

    def hi_of(name):
        if name in parts:
            return parts[name][:, 0]
        j = int(name[-1])
        return w1_hi[:, j] if name[1] == "1" else w2_hi[:, FC * j:FC * j + FC]

    def lo_of(name):
        if name in parts:
            return parts[name][:, 1]
        j = int(name[-1])
        return w1_lo[:, j] if name[1] == "1" else w2_lo[:, FC * j:FC * j + FC]

    block_cm = nc.Block()
    block = block_cm.__enter__()

    @block.sync
    def _(sp):
        def load_raw(name):
            buf, _ = raw_in[name]
            sp.dma_start(raw_buf[buf][:], raw_dram[name]).then_inc(raw_loaded[buf], 16)

        def load_stack(p, h):
            g, j = divmod(h, G)
            q, k = slice(j * DK, j * DK + DK), slot(h)
            if j == 0:
                sp.wait_ge(split["k" if g else "q"], p.n * G + (g + 1))
            elif not (p.first and h < G):
                sp.wait_ge(t_ready, p.chunk(h - G, TC))
            for i, (dst, src, part) in enumerate([(q_st, q_hl, 0), (q_st, q_hl, 1), (q_st, q_hl, 0),
                                                  (k_st, k_hl, 0), (k_st, k_hl, 0), (k_st, k_hl, 1)]):
                r = DK * (i % 3)
                sp.dma_start(dst[r:r + DK, k].bitcast(F32), src[q, part].bitcast(F32)).then_inc(stack_loaded[k], 16)

        def place_head(p, h):
            g, j = divmod(h, G)
            q = slice(j * DK, j * DK + DK)
            moved, joined = p.head(h + 1), p.n * G + g
            if g > 0 and not isinstance(p.n, int):
                moved, joined = sp.to_reg(moved), sp.to_reg(joined)
            sp.wait_ge(o_moved, moved)
            if g > 0:
                sp.wait_ge(o_joined, joined)
            if p.first and h == 0:
                sp.wait_ge(consts_set, 4)
                sp.wait_ge(w_split, 3)
            sp.dma_start(o_a[q], o_raw[0:DK, h % 2]).then_inc(o_placed[j], 16)
            sp.dma_start(o_b[q], o_raw[DK:2 * DK, h % 2]).then_inc(o_placed[j], 16)
            sp.dma_start(rs[q.start:q.start + 1], o_raw[2 * DK:2 * DK + 1, h % 2]).then_inc(o_placed[j], 16)

        def slot(h):
            return h % G

        def steps(p):
            for s in range(STEPS + 1):
                if s == 0 and not p.first:
                    sp.wait_ge(out_done, p.n * TC)
                    sp.wait_ge(stored, (p.n - 1) * 16)
                    sp.dma_start(xres[:], rows(x, p.n - 1)).then_inc(res_loaded, 16)
                if s >= 3 and s - 3 < NH:
                    place_head(p, s - 3)
                if s + 2 < NH:
                    load_stack(p, s + 2)
                if p.first:
                    if s == 0:
                        sp.wait_ge(split["v"], TC)
                        load_raw("wv")
                        sp.wait_ge(split["x"], FC)
                        load_raw("wq")
                        load_raw("wk")
                    if s == 2:
                        sp.wait_ge(w_split, 4)
                        load_raw("wo")
                    if s == 12:
                        sp.wait_ge(w_split, piece_no["wq"] + 1)
                        sp.dma_start(yt[:], rows(ctx, 0)).then_inc(y_loaded, 16)
                    if s == 16:
                        sp.wait_ge(unit_ready, p.unit("y", FC - 1) + 1)
                        sp.dma_start(yt[:], rows(x, 0)).then_inc(x_loaded, 16)
                elif not p.last:
                    if s == 2:
                        sp.wait_ge(unit_ready, p.n * PASS_UNITS + PRE_UNITS)
                        sp.dma_start(yt[:], rows(ctx, p.n)).then_inc(y_loaded, 16)
                    if s == 13:
                        sp.wait_ge(unit_ready, p.unit("y", FC - 1) + 1)
                        sp.dma_start(yt[:], rows(x, p.n)).then_inc(x_loaded, 16)
                else:
                    if s == 2:
                        sp.wait_ge(unit_ready, p.n * PASS_UNITS + PRE_UNITS)
                        sp.wait_ge(stored, 16)
                        sp.dma_start(yt[:], rows(x2, 0)).then_inc(x_loaded, 16)
                    if s == 4:
                        sp.wait_ge(res_summed, p.n)
                        load_raw("w1_0")
                    if s == 13:
                        sp.wait_ge(w_split, piece_no["w1_0"] + 1)
                        load_raw("w1_1")

        sp.dma_start(yt[:], rows(ctx, 0)).then_inc(y_loaded, 16)
        sp.dma_start(id_s[:], ident).then_inc(const_loaded, 16)
        sp.dma_start(col_s[:], cols).then_inc(const_loaded, 16)
        load_raw("l0wk")
        load_raw("l0wv")
        load_raw("l0wq")
        sp.dma_start(bp_s[:], bproj.partition_broadcast(P)).then_inc(const_loaded, 16)
        sp.dma_start(b2_s[:], b2.partition_broadcast(P)).then_inc(const_loaded, 16)
        sp.wait_ge(unit_ready, FC)
        sp.dma_start(yt[:], rows(x, 0)).then_inc(x_loaded, 16)
        load_stack(first, 0)
        load_stack(first, 1)
        steps(first)
        load_stack(Pass(1), 0)
        load_stack(Pass(1), 1)
        with sp.Fori(1, B) as i:
            p = Pass(i)
            steps(p)
            load_stack(Pass(i + 1), 0)
            load_stack(Pass(i + 1), 1)
            sp.wait_ge(out_done, (p.n + 1) * TC)
            sp.dma_start(rows(x2, p.n - 1), xres[:]).then_inc(stored, 16)
        steps(last)
        sp.wait_ge(o_joined, (B + 1) * G)
        load_raw("w2_0")
        sp.wait_ge(w_split, piece_no["w1_1"] + 1)
        load_raw("w1_2")
        sp.wait_ge(out_done, (B + 1) * TC)
        sp.dma_start(rows(x2, B - 1), xres[:]).then_inc(stored, 16)
        sp.wait_ge(w_split, piece_no["w2_0"] + 1)
        load_raw("w2_1")
        sp.wait_ge(stored, 16 * B)
        sp.dma_start(xres[:], rows(x2, 0)).then_inc(res_loaded, 16)
        sp.wait_ge(unit_ready, END_UNITS)
        sp.dma_start(yt[:], rows(x2, 1)).then_inc(x_loaded, 16)
        for name, before in (("w1_3", "w1_2"), ("w2_2", "w2_1"), ("w2_3", "w1_3")):
            sp.wait_ge(w_split, piece_no[before] + 1)
            load_raw(name)

        def store_tile(t):
            sp.wait_ge(out_done, t * TC + (B + 2) * TC)
            sp.dma_start(rows(out, t), xres[:]).then_inc(out_stored, 16)

        def load_tile(t, final):
            sp.wait_ge(out_stored, t * 16)
            sp.dma_start(xres[:], rows(x2, t)).then_inc(res_loaded, 16)
            if not final:
                sp.wait_ge(unit_ready, t * TILE_UNITS + END_UNITS)
                sp.dma_start(yt[:], rows(x2, t + 1)).then_inc(x_loaded, 16)

        store_tile(0)
        with sp.Fori(1, B - 1) as i:
            load_tile(i, False)
            store_tile(i)
        load_tile(B - 1, True)
        store_tile(B - 1)
        sp.wait_ge(out_stored, 16 * B)

    @block.tensor
    def _(pe):
        taken = {0: [], 1: []}

        def bank(p, kind, c):
            b = p.bank(kind, c)
            for s, value in taken[b]:
                pe.wait_ge(s, value)
            return ps_d[:, b]

        def filled(ins, p, kind, c, s, value):
            ins.then_inc(unit_ready, 1)
            taken[p.bank(kind, c)] = [(s, value)]

        def transposes(p, kind, c, src, k):
            dst = bank(p, kind, c)
            for t in range(TC):
                ins = nc.tensor.transpose(dst[:, t * P:t * P + P], src[:, t, c * P:c * P + P], id_s[:])
            filled(ins, p, kind, c, split[kind], k + (c + 1))

        def products(dst, lhs, rhs, chunks):
            for c in range(chunks):
                for n, (a, b) in enumerate(((0, 0), (0, 1), (1, 0))):
                    ins = nc.tensor.matmul(dst, lhs(a, c), rhs(b, c), start=(c == 0 and n == 0),
                                           stop=(c == chunks - 1 and n == 2))
            return ins

        def project(p, kind, g, w, src, k):
            dst = bank(p, kind, g)
            ins = products(dst, lambda a, c: w[:, a, c, (g % G) * P:(g % G) * P + P],
                           lambda b, c: src[:, b, c], FC)
            filled(ins, p, kind, g, split[kind], k)

        def q_project(p, g):
            project(p, "q", g, wq_s, xT, p_of(p) * G + (g + 1))

        def k_project(p, g):
            project(p, "k", g, wk_s, yT, p_of(p) * G + (g + 1))

        def p_of(p):
            return 0 if isinstance(p, Before) else p.n

        def v_project(p, n):
            for t in range(TC):
                dst = bank(p, "v", t)
                ins = products(dst, lambda a, c: yT[:, a, c, t * P:t * P + P],
                               lambda b, c: wv_s[:, b, c], FC)
                filled(ins, p, "v", t, split["v"], n * TC + (t + 1))

        def steps(p):
            for s in range(STEPS):
                h_s, h_t, h_v = s, s - 1, s - 2

                def scores(c):
                    if h_s >= NH:
                        return
                    if c == 0:
                        pe.wait_ge(stack_loaded[h_s % G], (p.n * G + (h_s // G + 1)) * (16 * STACK_DMAS))
                    if not (p.first and h_s == 0 and c < 2):
                        pe.wait_ge(s_maxed, p.chunk(h_s, c - 1))
                    nc.tensor.matmul(ps_s[:, c % 2], q_st[0:KQ, h_s % G, c * P:c * P + P],
                                     k_st[0:KQ, h_s % G], start=True, stop=True).then_inc(s_ready, 1)

                def spread_max():
                    if not 0 <= h_t < NH:
                        return
                    pe.wait_ge(s_maxed, p.chunk(h_t, TC))
                    if not (p.first and h_t == 0):
                        pe.wait_ge(m_moved, p.head(h_t))
                    else:
                        pe.wait_ge(ident_set, 1)
                    for c in range(TC):
                        ins = nc.tensor.matmul(ps_m[:, c * P:c * P + P],
                                               negmax[:, h_t % 2, c:c + 1].broadcast_to([P, P]),
                                               id_r[:], start=True, stop=True)
                    ins.then_inc(m_spread, 1)

                def shifted(c):
                    if not 0 <= h_t < NH:
                        return
                    if c == 0:
                        pe.wait_ge(m_moved, p.head(h_t + 1))
                        if p.first and h_t == 0:
                            pe.wait_ge(consts_set, 1)
                    if not (p.first and h_t == 0 and c < 2):
                        pe.wait_ge(p_split, p.chunk(h_t, c - 1))
                    nc.tensor.matmul(ps_t[:, c % 2], k_st[0:KM, h_t % G, c * P:c * P + P],
                                     q_st[0:KM, h_t % G], start=True, stop=True).then_inc(t_ready, 1)

                def weigh(c):
                    if not 0 <= h_v < NH:
                        return
                    if c == 0:
                        if not (p.first and h_v == 0):
                            pe.wait_ge(o_moved, p.head(h_v))
                        if h_v == 0:
                            pe.wait_ge(split["v"], (p.n + 1) * TC)
                            if p.first:
                                pe.wait_ge(consts_set, 2)
                    pe.wait_ge(p_split, p.chunk(h_v, c + 1))
                    for n, src in enumerate((p_hi, p_lo)):
                        ins = nc.tensor.matmul(ps_o[0:VW], v_s[:, c, h_v], src[:, c],
                                               start=(c == 0 and n == 0), stop=(c == TC - 1 and n == 1))
                    ins.then_inc(pv_done, 1)

                spread_max()
                scores(0)
                scores(1)
                weigh(0)
                weigh(1)
                shifted(0)
                scores(2)
                shifted(1)
                weigh(2)
                scores(3)
                shifted(2)
                weigh(3)
                shifted(3)

                if s % G == 1 and s // G + 1 < FC:
                    if s == 1:
                        busy = [(split["q"], p.n * G + 1), (split["v"], (p.n + 1) * TC)]
                        if not p.first:
                            busy.append((out_done, p.n * TC))
                        taken[0], taken[1] = list(busy), list(busy)
                    q_project(p, s // G + 1)
                if s % G == 2 and s // G + 1 < FC:
                    k_project(p, s // G + 1)
                if p.first:
                    if s == 14:
                        pe.wait_ge(normed, 1)
                        for c in range(FC):
                            transposes(p, "y", c, yt, FC)
                    if s == 16:
                        pe.wait_ge(w_split, piece_no["wk"] + 1)
                        pe.wait_ge(split["y"], 2 * FC)
                        k_project(p, G)
                elif not p.last:
                    if s == 12:
                        pe.wait_ge(normed, p.n * 2 + 1)
                        for c in range(FC):
                            transposes(p, "y", c, yt, (p.n + 1) * FC)
                    if s == 14:
                        pe.wait_ge(split["y"], (p.n + 2) * FC)
                        k_project(p, G)
                    if s == 16:
                        pe.wait_ge(normed, p.n * 2 + 2)
                        for c in range(FC):
                            transposes(p, "x", c, yt, (p.n + 1) * FC)
                    if s == 17:
                        pe.wait_ge(split["x"], (p.n + 2) * FC)
                        q_project(p, G)
                elif s == 12:
                    pe.wait_ge(normed, 2 * B + 1)
                    for c in range(FC):
                        transposes(p, "h", c, yt, 0)

        def project_out(p):
            pe.wait_ge(o_joined, (p.n + 1) * G)
            for t in range(TC):
                dst = bank(p, "out", t)
                ins = products(dst, lambda a, c: oT[:, a, c, t * P:t * P + P],
                               lambda b, c: wo_s[:, b, c], FC)
                filled(ins, p, "out", t, out_done, p.n * TC + (t + 1))

        pre = Before()
        pe.wait_ge(y_loaded, 16)
        pe.wait_ge(const_loaded, 64)
        for c in range(FC):
            transposes(pre, "y", c, yt, 0)
        pe.wait_ge(split["y"], FC)
        pe.wait_ge(w_split, 2)
        v_project(pre, 0)
        k_project(pre, 0)
        pe.wait_ge(x_loaded, 16)
        for c in range(FC):
            transposes(pre, "x", c, yt, 0)
        pe.wait_ge(split["x"], FC)
        pe.wait_ge(w_split, 3)
        q_project(pre, 0)

        steps(first)
        pe.wait_ge(w_split, piece_no["wk"] + 1)
        v_project(first, 1)
        pe.wait_ge(o_joined, G)
        for t in range(TC):
            dst = bank(first, "out", t)
            for c in range(FC):
                ins = nc.tensor.transpose(dst[:, c * P:c * P + P], xres[:, c, t * P:t * P + P], id_s[:])
            filled(ins, first, "out", t, out_done, t + 1)
        pe.wait_ge(normed, 2)
        for c in range(FC):
            transposes(first, "x", c, yt, FC)
        pe.wait_ge(split["x"], 2 * FC)
        q_project(first, G)

        with pe.Fori(1, B) as i:
            p = Pass(i)
            steps(p)
            v_project(p, p.n + 1)
            project_out(p)
        steps(last)
        project_out(last)

        def hidden(t, c):
            b = c % 2
            if c == 0:
                pe.wait_ge(split["h"], (t + 1) * FC)
                if isinstance(t, int) and t == 0:
                    pe.wait_ge(out_done, (B + 1) * TC)
            if c >= 2:
                pe.wait_ge(split["g"], t * HC + (c - 1))
            if isinstance(t, int) and t == 0 and c % FC == 0:
                pe.wait_ge(w_split, piece_no[f"w1_{c // FC}"] + 1)
            q, j = divmod(c, FC)
            w = (w1_hi, w1_lo)
            ins = products(ps_d[:, b], lambda a, k: w[a][:, q, k, j * P:j * P + P],
                           lambda b, k: xT[:, b, k], FC)
            ins.then_inc(unit_ready, 1)

        def output(t, c):
            if c == 0 and not (isinstance(t, int) and t == 0):
                pe.wait_ge(out_done, (t + (B + 1)) * TC)
            if isinstance(t, int) and t == 0 and c % FC == 0:
                pe.wait_ge(w_split, piece_no[f"w2_{c // FC}"] + 1)
            pe.wait_ge(split["g"], t * HC + (c + 1))
            g, w = (p_hi, p_lo), (w2_hi, w2_lo)
            for k in range(TC):
                for n, (a, b) in enumerate(((0, 0), (0, 1), (1, 0))):
                    ins = nc.tensor.matmul(out_banks[k], g[a][:, c % TC, k * P:k * P + P], w[b][:, c],
                                           start=(c == 0 and n == 0), stop=(c == HC - 1 and n == 2))
            ins.then_inc(y2_done, 1)

        def tile(t, final):
            for c in range(HC):
                hidden(t, c)
                if c == HC - 1 and not final:
                    pe.wait_ge(normed, t + (2 * B + 2))
                    for k in range(FC):
                        if k < 2:
                            pe.wait_ge(split["g"], t * HC + (HC - 1 + k))
                        else:
                            pe.wait_ge(split["h"], t * FC + (FC + k - 1))
                        for r in range(TC):
                            ins = nc.tensor.transpose(ps_d[:, k % 2, r * P:r * P + P],
                                                      yt[:, r, k * P:k * P + P], id_s[:])
                        ins.then_inc(unit_ready, 1)
                if c >= 1:
                    output(t, c - 1)
            output(t, HC - 1)

        tile(0, False)
        with pe.Fori(1, B - 1) as i:
            tile(i, False)
        tile(B - 1, True)

    @block.scalar
    def _(act):
        def hi_weights(name):
            buf, use = raw_in[name]
            act.wait_ge(raw_loaded[buf], 16 * use)
            act.activation(hi_of(name), raw_buf[buf][:], ACT.Identity).then_inc(w_hi, 1)

        def hi_plain(p, kind, c, dst, src):
            act.wait_ge(unit_ready, p.unit(kind, c) + 1)
            act.activation(dst, src, ACT.Identity).then_inc(hi_ready, 1)

        def hi_affine(p, kind, c, dst, gain, bias):
            act.wait_ge(unit_ready, p.unit(kind, c) + 1)
            b = ps_d[:, p.bank(kind, c)]
            act.activation(dst, b, ACT.Identity, bias=col(bias, c), scale=col(gain, c))
            act.activation(b, b, ACT.Identity, bias=col(bias, c), scale=col(gain, c)).then_inc(hi_ready, 1)

        def hi_heads(p, q, kind, g):
            if not (q.first and g == 0):
                for j in range(G):
                    act.wait_ge(stack_loaded[j], (q.n * G + g) * (16 * STACK_DMAS))
            dst = q_hl if kind == "q" else k_hl
            src = ps_d[:, p.bank(kind, g if p is q else (0 if isinstance(p, Before) else G))]
            hi_plain(p, kind, g if p is q else (0 if isinstance(p, Before) else G), dst[:, 0], src)

        def hi_values(p):
            for t in range(TC):
                hi_plain(p, "v", t, v_s[:, t, :, 0:DK],
                         ps_d[:, p.bank("v", t)].rearrange("p (h d) -> p h d", h=NH))

        def steps(p):
            nxt = None if p.last else Pass(p.n + 1)
            for s in range(STEPS):
                h_t, h_v = s - 1, s - 2
                if 0 <= h_t < NH:
                    act.wait_ge(m_spread, p.head(h_t + 1))
                    act.activation(q_st[KQ:KM, h_t % G], ps_m[KQ:KM], ACT.Identity).then_inc(m_moved, 1)
                    for c in range(TC):
                        act.wait_ge(t_ready, p.chunk(h_t, c + 1))
                        if not (p.first and h_t == 0):
                            act.wait_ge(pv_done, p.chunk(h_t - 1, c + 1))
                        act.activation(p_hi[:, c], ps_t[:, c % 2], ACT.Exp, scale=SCALE)
                        act.activation(ps_t[:, c % 2], ps_t[:, c % 2], ACT.Exp, scale=SCALE).then_inc(p_exp, 1)
                if 0 <= h_v < NH:
                    act.wait_ge(pv_done, p.chunk(h_v, TC))
                    if not (p.first and h_v < 2):
                        act.wait_ge(o_placed[(h_v - 2) % G], (p.n * G + ((h_v - 2) // G + 1)) * (16 * PLACE_DMAS))
                    act.activation(o_raw[0:VW, h_v % 2], ps_o[0:VW], ACT.Identity).then_inc(o_moved, 1)
                if s % G == 1 and s // G + 1 < FC:
                    hi_heads(p, p, "q", s // G + 1)
                if s % G == 2 and s // G + 1 < FC:
                    hi_heads(p, p, "k", s // G + 1)
                if p.first:
                    if s == 2:
                        act.wait_ge(split["v"], TC)
                        hi_weights("wv")
                    if s == 4:
                        hi_weights("wo")
                    if s == 11:
                        act.wait_ge(unit_ready, p.unit("k", 3) + 1)
                        hi_weights("wq")
                        hi_weights("wk")
                    if s == 14:
                        for c in range(FC):
                            hi_affine(p, "y", c, yT[:, 0, c], GKV, BKV)
                    if s == 16:
                        hi_heads(p, nxt, "k", 0)
                elif not p.last:
                    if s == 12:
                        for c in range(FC):
                            hi_affine(p, "y", c, yT[:, 0, c], GKV, BKV)
                    if s == 14:
                        hi_heads(p, nxt, "k", 0)
                    if s == 16:
                        for c in range(FC):
                            hi_affine(p, "x", c, xT[:, 0, c], GQ, BQ)
                    if s == 17:
                        hi_heads(p, nxt, "q", 0)
                else:
                    if s == 12:
                        for c in range(FC):
                            hi_affine(p, "h", c, xT[:, 0, c], GM, BM)
                        hi_weights("w1_0")
                    if s == 16:
                        hi_weights("w1_1")

        pre = Before()
        act.wait_ge(const_loaded, 64)
        act.activation(id_r[:], id_s[:], ACT.Identity).then_inc(ident_set, 1)
        for name in ("l0wk", "l0wv", "l0wq"):
            hi_weights(name)
        for c in range(FC):
            hi_plain(pre, "y", c, yT[:, 0, c], ps_d[:, pre.bank("y", c)])
        hi_values(pre)
        hi_heads(pre, first, "k", 0)
        for c in range(FC):
            hi_plain(pre, "x", c, xT[:, 0, c], ps_d[:, pre.bank("x", c)])
        hi_heads(pre, first, "q", 0)
        steps(first)
        hi_values(first)
        for c in range(FC):
            hi_affine(first, "x", c, xT[:, 0, c], GQ, BQ)
        hi_heads(first, Pass(1), "q", 0)
        with act.Fori(1, B) as i:
            p = Pass(i)
            steps(p)
            hi_values(p)
        steps(last)

        def tile(t, final):
            for c in range(HC):
                if isinstance(t, int) and t == 0 and c in (0, 1, 4, 6, 8, 10):
                    name = {0: "w2_0", 1: "w1_2", 4: "w2_1", 6: "w1_3", 8: "w2_2", 10: "w2_3"}[c]
                    if c == 0:
                        act.wait_ge(unit_ready, END_UNITS)
                    hi_weights(name)
                act.wait_ge(unit_ready, t * TILE_UNITS + (END_UNITS + c + 1))
                if not (isinstance(t, int) and t == 0 and c < TC):
                    act.wait_ge(y2_done, t * HC + (c - TC + 1))
                else:
                    act.wait_ge(pv_done, (B + 1) * CH)
                b1 = col_s[:, 6 * FC + c:6 * FC + c + 1]
                act.activation(p_hi[:, c % TC], ps_d[:, c % 2], ACT.Gelu, bias=b1)
                act.activation(ps_d[:, c % 2], ps_d[:, c % 2], ACT.Gelu, bias=b1).then_inc(hi_ready, 1)
            if not final:
                for k in range(FC):
                    act.wait_ge(unit_ready, t * TILE_UNITS + (END_UNITS + HC + k + 1))
                    b = ps_d[:, k % 2]
                    act.activation(xT[:, 0, k], b, ACT.Identity, bias=col(BM, k), scale=col(GM, k))
                    act.activation(b, b, ACT.Identity, bias=col(BM, k), scale=col(GM, k)).then_inc(hi_ready, 1)

        tile(0, False)
        with act.Fori(1, B - 1) as i:
            tile(i, False)
        tile(B - 1, True)

    @block.vector
    def _(dve):
        def lo(p, kind, c, dst, src, hi):
            dve.wait_ge(hi_ready, p.split(kind, c) + 1)
            dve.tensor_tensor(dst, src, hi, ALU.subtract).then_inc(split[kind], 1)

        def lo_chunks(p, kind, dst):
            for c in range(FC):
                lo(p, kind, c, dst[:, 1, c], ps_d[:, p.bank(kind, c)], dst[:, 0, c].bitcast(F32))

        def lo_heads(p, kind, g):
            dst = q_hl if kind == "q" else k_hl
            lo(p, kind, g, dst[:, 1], ps_d[:, p.bank(kind, g)], dst[:, 0].bitcast(F32))

        def lo_values(p):
            for t in range(TC):
                lo(p, "v", t, v_s[:, t, :, DK:2 * DK],
                   ps_d[:, p.bank("v", t)].rearrange("p (h d) -> p h d", h=NH),
                   v_s[:, t, :, 0:DK].bitcast(F32))

        def norm_stats(n):
            for t in range(TC):
                dve.bn_stats(stats[:, t], yt[:, t])
            dve.drain()
            for t in range(TC):
                ins = dve.bn_aggr(mv[:, t], stats[:, t])
            ins.then_inc(ln_var, 1)

        def norm_apply(n):
            dve.wait_ge(ln_rstd, n + 1)
            for t in range(TC):
                ins = dve.tensor_scalar(yt[:, t], yt[:, t], mv[:, t, 0:1], rstd[:, t:t + 1],
                                        ALU.subtract, ALU.mult)
            ins.then_inc(normed, 1)

        def invert(p, g):
            for j in range(G):
                dve.wait_ge(o_placed[j], (p.n * G + (g + 1)) * (16 * PLACE_DMAS))
            own = (p.n * G + g) * 2
            dve.transpose(rs_t[:], rs[:]).then_inc(inv_own, 1)
            dve.wait_ge(inv_own, own + 1)
            sums = rs_t[:].rearrange("p (b e) -> p b e", e=DK)[:, :, 0]
            dve.reciprocal(rinv[:], sums).then_inc(inv_own, 1)
            dve.wait_ge(inv_own, own + 2)
            dve.tensor_copy(rs_t[:].rearrange("p (b e) -> p b e", e=DK),
                            rinv[:].unsqueeze(2).broadcast_to([P, T // DK, DK])).then_inc(inv_copied, 1)
            dve.wait_ge(inv_copied, p.n * G + (g + 1))
            dve.transpose(rs[:], rs_t[:]).then_inc(inv_ready, 1)

        def steps(p):
            for s in range(STEPS):
                h_s, h_t = s, s - 1

                def maxima(c):
                    if h_s >= NH:
                        return
                    dve.wait_ge(s_ready, p.chunk(h_s, c + 1))
                    if c == 0 and not (p.first and h_s < 2):
                        dve.wait_ge(m_spread, p.head(h_s - 1))
                    dve.tensor_reduce(negmax[:, h_s % 2, c:c + 1], ps_s[:, c % 2], AX.X, ALU.max,
                                      negate=True).then_inc(s_maxed, 1)

                def lo_probs(c):
                    if not 0 <= h_t < NH:
                        return
                    dve.wait_ge(p_exp, p.chunk(h_t, c + 1))
                    dve.tensor_tensor(p_lo[:, c], ps_t[:, c % 2], p_hi[:, c].bitcast(F32),
                                      ALU.subtract).then_inc(p_split, 1)

                maxima(0)
                maxima(1)
                lo_probs(0)
                maxima(2)
                lo_probs(1)
                maxima(3)
                lo_probs(2)
                lo_probs(3)
                if s % G == 2 and s >= 6:
                    invert(p, s // G - 1)
                if s % G == 1 and s // G + 1 < FC:
                    lo_heads(p, "q", s // G + 1)
                if s % G == 2 and s // G + 1 < FC:
                    lo_heads(p, "k", s // G + 1)
                if p.first:
                    if s == 13:
                        dve.wait_ge(y_loaded, 32)
                        norm_stats(0)
                    if s == 14:
                        norm_apply(0)
                        lo_chunks(p, "y", yT)
                    if s == 16:
                        lo_heads(p, "k", G)
                elif not p.last:
                    if s == 8:
                        dve.wait_ge(y_loaded, (p.n + 2) * 16)
                        norm_stats(p.n * 2)
                    if s == 9:
                        norm_apply(p.n * 2)
                    if s == 12:
                        lo_chunks(p, "y", yT)
                    if s == 14:
                        lo_heads(p, "k", G)
                    if s == 15:
                        dve.wait_ge(x_summed, p.n + 1)
                        norm_stats(p.n * 2 + 1)
                        norm_apply(p.n * 2 + 1)
                    if s == 16:
                        lo_chunks(p, "x", xT)
                    if s == 17:
                        lo_heads(p, "q", G)
                else:
                    if s == 8:
                        dve.wait_ge(x_loaded, (B + 2) * 16)
                        norm_stats(2 * B)
                    if s == 9:
                        norm_apply(2 * B)
                    if s == 12:
                        lo_chunks(p, "h", xT)

        def residual(p):
            dve.wait_ge(res_summed, p.n)
            for t in range(TC):
                dve.wait_ge(unit_ready, p.unit("out", t) + 1)
                dve.tensor_tensor(xres[:, t], ps_d[:, p.bank("out", t)], xres[:, t], ALU.add)\
                   .then_inc(out_done, 1)

        dve.memset(k_st[KQ:KM].bitcast(F32), 1.0).then_inc(consts_set, 1)
        dve.memset(v_s[:, :, :, 2 * DK:VW].bitcast(F32), 1.0).then_inc(consts_set, 1)
        pre = Before()
        for c in range(FC):
            lo(pre, "y", c, yT[:, 1, c], ps_d[:, pre.bank("y", c)], yT[:, 0, c].bitcast(F32))
        lo_values(pre)
        lo_heads(pre, "k", 0)
        lo_chunks(pre, "x", xT)
        lo_heads(pre, "q", 0)
        dve.wait_ge(w_split, 3)
        dve.memset(rs[:], 1.0).then_inc(consts_set, 1)
        dve.memset(rs_t[:], 1.0).then_inc(consts_set, 1)
        steps(first)
        lo_values(first)
        invert(first, G - 1)
        for t in range(TC):
            dve.wait_ge(unit_ready, first.unit("out", t) + 1)
            if t == 0:
                dve.wait_ge(w_split, piece_no["wk"] + 1)
            dve.tensor_copy(tgt2[:, t], ps_d[:, first.bank("out", t)]).then_inc(out_done, 1)
        dve.wait_ge(x_summed, 1)
        norm_stats(1)
        norm_apply(1)
        lo_chunks(first, "x", xT)
        lo_heads(first, "q", G)
        with dve.Fori(1, B) as i:
            p = Pass(i)
            steps(p)
            invert(p, G - 1)
            lo_values(p)
            residual(p)
        steps(last)
        invert(last, G - 1)
        residual(last)

        def tile(t, final):
            for c in range(HC):
                dve.wait_ge(hi_ready, t * TILE_UNITS + (END_SPLITS + c + 1))
                dve.tensor_tensor(p_lo[:, c % TC], ps_d[:, c % 2], p_hi[:, c % TC].bitcast(F32),
                                  ALU.subtract).then_inc(split["g"], 1)
                if c == 8 and not final:
                    dve.wait_ge(x_loaded, (t + (B + 3)) * 16)
                    norm_stats(t + (2 * B + 1))
                if c == 9 and not final:
                    norm_apply(t + (2 * B + 1))
            if not final:
                for k in range(FC):
                    dve.wait_ge(hi_ready, t * TILE_UNITS + (END_SPLITS + HC + k + 1))
                    dve.tensor_tensor(xT[:, 1, k], ps_d[:, k % 2], xT[:, 0, k].bitcast(F32),
                                      ALU.subtract).then_inc(split["h"], 1)
            dve.wait_ge(y2_done, (t + 1) * HC)
            dve.wait_ge(res_summed, t + (B + 1))
            for k in range(TC):
                dve.tensor_tensor(xres[:, k], out_banks[k], xres[:, k], ALU.add).then_inc(out_done, 1)

        tile(0, False)
        with dve.Fori(1, B - 1) as i:
            tile(i, False)
        tile(B - 1, True)

    @block.gpsimd
    def _(pool):
        def lo_weights(name):
            buf, _ = raw_in[name]
            pool.wait_ge(w_hi, piece_no[name] + 1)
            pool.tensor_tensor(lo_of(name), raw_buf[buf][:], hi_of(name).bitcast(F32), ALU.subtract)\
                .then_inc(w_split, 1)

        def norm_rstd(n):
            pool.wait_ge(ln_var, n + 1)
            pool.tensor_tensor(var_e[:], mv[:, :, 1], eps_s[:], ALU.add).then_inc(ln_eps, 1)
            pool.wait_ge(ln_eps, n + 1)
            pool.tensor_tensor(rstd[:], var_e[:], m_half[:], ALU.pow).then_inc(ln_rstd, 1)

        def join(p, g):
            own = (p.n * G + g) * 3
            for j in range(G):
                pool.wait_ge(o_placed[j], (p.n * G + (g + 1)) * (16 * PLACE_DMAS))
            pool.tensor_tensor(o_a[:], o_a[:], o_b[:], ALU.add).then_inc(join_own, 1)
            pool.wait_ge(join_own, own + 1)
            pool.wait_ge(inv_ready, p.n * G + (g + 1))
            if p.first:
                if g == 0:
                    pool.wait_ge(w_split, piece_no["wo"] + 1)
                pool.tensor_tensor(xres[:, g], o_a[:], rs[:], ALU.mult).then_inc(o_joined, 1)
                pool.sem_inc(join_own, 2)
            else:
                pool.tensor_tensor(oT[:, 0, g], o_a[:], rs[:], ALU.mult).then_inc(join_own, 1)
                pool.tensor_tensor(o_a[:], o_a[:], rs[:], ALU.mult).then_inc(join_own, 1)
                pool.wait_ge(join_own, own + 3)
                pool.tensor_tensor(oT[:, 1, g], o_a[:], oT[:, 0, g].bitcast(F32), ALU.subtract)\
                    .then_inc(o_joined, 1)

        def steps(p):
            for s in range(STEPS):
                if s == 2 and not p.first:
                    pool.wait_ge(res_loaded, p.n * 16)
                    pool.tensor_tensor(xres[:], xres[:], tgt2[:], ALU.add).then_inc(res_own, 1)
                    pool.wait_ge(res_own, p.n)
                    pool.tensor_tensor(xres[:], xres[:], bp_s[:].unsqueeze(1).broadcast_to([P, TC, D]),
                                       ALU.add).then_inc(res_summed, 1)
                if s == 14 and not p.first and not p.last:
                    pool.wait_ge(x_loaded, (p.n + 2) * 16)
                    pool.tensor_tensor(yt[:], yt[:], tgt2[:], ALU.add).then_inc(x_summed, 1)
                if s % G == 2 and s >= 6:
                    join(p, s // G - 1)
                if p.first:
                    if s == 2:
                        lo_weights("wv")
                    if s == 4:
                        lo_weights("wo")
                    if s == 11:
                        lo_weights("wq")
                        lo_weights("wk")
                    if s == 13:
                        norm_rstd(0)
                elif not p.last:
                    if s == 8:
                        norm_rstd(p.n * 2)
                    if s == 14:
                        norm_rstd(p.n * 2 + 1)
                else:
                    if s == 8:
                        norm_rstd(2 * B)
                    if s == 12:
                        lo_weights("w1_0")
                    if s == 16:
                        lo_weights("w1_1")

        pool.memset(m_half[:], -0.5).then_inc(half_set, 1)
        pool.memset(eps_s[:], EPS).then_inc(half_set, 1)
        pool.wait_ge(half_set, 2)
        for name in ("l0wk", "l0wv", "l0wq"):
            lo_weights(name)
        steps(first)
        join(first, G - 1)
        pool.wait_ge(x_loaded, 32)
        pool.wait_ge(out_done, TC)
        pool.tensor_tensor(yt[:], yt[:], tgt2[:], ALU.add).then_inc(x_summed, 1)
        norm_rstd(1)
        with pool.Fori(1, B) as i:
            p = Pass(i)
            steps(p)
            join(p, G - 1)
        steps(last)
        join(last, G - 1)

        def add_bias(t):
            pool.wait_ge(res_loaded, (t + (B + 1)) * 16)
            pool.tensor_tensor(xres[:], xres[:], b2_s[:].unsqueeze(1).broadcast_to([P, TC, D]),
                               ALU.add).then_inc(res_summed, 1)

        for name in ("w2_0", "w1_2", "w2_1"):
            lo_weights(name)
        add_bias(0)
        for name in ("w1_3", "w2_2", "w2_3"):
            lo_weights(name)
        norm_rstd(2 * B + 1)
        with pool.Fori(1, B - 1) as i:
            add_bias(i)
            norm_rstd(i + (2 * B + 1))
        add_bias(B - 1)

    block_cm.__exit__(None, None, None)


def kernel(x, ctx_1024, L0_xattn_Wq, L0_xattn_Wk, L0_xattn_Wv, L1_xattn_gq, L1_xattn_bq, L1_xattn_gkv,
           L1_xattn_bkv, L1_xattn_Wq, L1_xattn_Wkv, L1_xattn_Wproj, L1_xattn_bproj, L1_xattn_gm,
           L1_xattn_bm, L1_xattn_W1, L1_xattn_b1, L1_xattn_W2, L1_xattn_b2):
    import concourse.bacc as bacc
    from concourse.bass_utils import run_bass_kernel_spmd

    def chunked(w):
        w = np.asarray(w)
        return np.ascontiguousarray(w.reshape(-1, P, w.shape[1]).transpose(1, 0, 2))

    def columns(v):
        return np.asarray(v).reshape(-1, P).T

    wkv = np.asarray(L1_xattn_Wkv)
    w1 = np.asarray(L1_xattn_W1).reshape(FC, P, FC, D).transpose(2, 1, 0, 3)
    arrays = {
        "x": np.ascontiguousarray(x),
        "ctx": np.ascontiguousarray(ctx_1024),
        "l0wq": chunked(np.asarray(L0_xattn_Wq).T),
        "l0wk": chunked(np.asarray(L0_xattn_Wk).T),
        "l0wv": chunked(np.asarray(L0_xattn_Wv).T),
        "wq": chunked(L1_xattn_Wq),
        "wk": chunked(wkv[:, :D]),
        "wv": chunked(wkv[:, D:]),
        "wo": chunked(L1_xattn_Wproj),
        "w1": np.ascontiguousarray(w1),
        "w2": chunked(L1_xattn_W2),
        "cols": np.ascontiguousarray(np.concatenate(
            [columns(v) for v in (L1_xattn_gq, L1_xattn_bq, L1_xattn_gkv, L1_xattn_bkv, L1_xattn_gm,
                                  L1_xattn_bm, L1_xattn_b1)], axis=1)),
        "bproj": np.ascontiguousarray(L1_xattn_bproj),
        "b2": np.ascontiguousarray(L1_xattn_b2),
        "ident": np.eye(P, dtype=np.float32),
    }
    nc = bacc.Bacc("TRN2", target_bir_lowering=False, num_devices=1, dynamic_dma_scratch_size=1024)
    args = [nc.dram_tensor(name, a.shape, mybir.dt.from_np(a.dtype), kind="ExternalInput").ap()
            for name, a in arrays.items()]
    out = nc.dram_tensor("out", (B, T, D), F32, kind="ExternalOutput").ap()
    xattn_program(nc, *args, out)
    r = run_bass_kernel_spmd(nc, [arrays], core_ids=[0])
    return r.results[0]["out"]
```

```python
import numpy as np

import concourse.bass as bass
from concourse import mybir

F32 = mybir.dt.float32
F32R = mybir.dt.float32r
ACT = mybir.ActivationFunctionType
ALU = mybir.AluOpType
AX = mybir.AxisListType

P = 128
T = 512
D = 512
F = 2048
B = 8
NH = 16
DK = D // NH
FC = D // P
TC = T // P
HC = F // P
G = P // DK
SCALE = float(DK) ** -0.5
EPS = 1e-5

KQ = 3 * DK
KM = KQ + 1
VW = 2 * DK + 1
STEPS = NH + 2
CH = NH * TC
STACK_DMAS = 4
PLACE_DMAS = 2
NCOLS = 6 * FC + HC

SHIFT_LAG = 6
WEIGH_LAG = 8
SPREAD_AT = TC
MAXIMA_AT = SPREAD_AT + 1
MOVE_AT = TC - 1 + WEIGH_LAG
INVERT_AT = 26
DRAIN = 18
STACK_AHEAD = 6

PLAN = [
    (("v", 0), (4, 4, 5, 5)), (("v", 1), (5, 6, 6, 6)), (("v", 2), (7, 7, 7, 8)), (("v", 3), (8, 8, 9, 9)),
    (("q", 1), (10, 10, 11, 11)), (("k", 2), (12, 13, 14, 15)),
    (("out", 0), (16, 17, 17, 18)), (("out", 1), (19, 20, 20, 21)), (("q", 2), (21, 22, 23, 23)),
    (("out", 2), (24, 25, 25, 26)), (("out", 3), (26, 27, 27, 28)), (("k", 3), (29, 30, 31, 32)),
    (("y", 0), (33,)), (("y", 1), (34,)), (("y", 2), (36,)), (("y", 3), (37,)),
    (("q", 3), (38, 39, 39, 40)),
    (("x", 0), (41,)), (("x", 1), (42,)), (("k", 4), (43, 44, 44, 45)), (("x", 2), (46,)), (("x", 3), (48,)),
    (("q", 4), (50, 51, 52, 53)), (("k", 5), (58, 59, 60, 61)),
]


class Pass:

    def __init__(self, n, kind="steady"):
        self.n = n
        self.first, self.cold, self.last = kind == "first", kind == "cold", kind == "last"
        self.follows = kind in ("steady", "last")
        self.quarters = CH + (DRAIN if self.first or self.last else 0)
        if self.first:
            plan = [u for u in PLAN if u[0][0] in "yqk" and u[0] != ("q", G)]
            after = [("v", c) for c in range(TC)] + [("out", c) for c in range(TC)]
            after += [("x", c) for c in range(FC)] + [("q", G)]
        elif self.cold:
            plan, after = [u for u in PLAN if u[0][0] not in ("v", "out")], []
        elif self.last:
            plan = [(("h", u[0][1]), u[1]) if u[0][0] == "x" else u for u in PLAN
                    if u[0][0] != "y" and not (u[0][0] in "qk" and u[0][1] >= G)]
            after = [("end", c) for c in range(TC)]
        else:
            plan, after = PLAN, []
        order = [u for u, _ in plan] + after
        self.no = {u: i for i, u in enumerate(order)}
        self.units = len(order)
        split = [u for u in order if u[0] not in ("out", "end")]
        self.split_no = {u: i for i, u in enumerate(split)}
        self.splits = len(split)
        self.parts, self.his, self.los = {}, {}, {}
        for (kind, c), quarters in plan:
            for i, k in enumerate(quarters):
                self.parts.setdefault(k, []).append((kind, c, i))
            hi = quarters[-1]
            if kind == "q" and c > 1:
                hi = max(hi, TC * G * (c - 1) + SHIFT_LAG + 2)
            if kind != "out":
                self.his.setdefault(hi, []).append((kind, c))
            self.los.setdefault(hi + 1, []).append((kind, c))

    def base(self, steady, before):
        if isinstance(self.n, int) and self.n < 2:
            return before[self.n]
        return (self.n - 2) * steady + before[2]

    def unit(self, kind, c):
        return self.base(len(PLAN), UNITS_BEFORE) + self.no[kind, c]

    def split(self, kind, c):
        return self.base(len(PLAN) - TC, SPLITS_BEFORE) + self.split_no[kind, c]

    def bank(self, kind, c):
        return (UNITS_BEFORE[2] + self.no[kind, c]) % 2

    def chunk(self, c):
        return self.n * CH + c if c >= 0 else self.n * CH - (-c)

    def head(self, h):
        return self.n * NH + h if h >= 0 else self.n * NH - (-h)

    def runs(self, c):
        return c < CH and (c >= 0 or self.follows)


class Before:

    n, first = 0, True
    order = [("y", c) for c in range(FC)] + [("v", c) for c in range(TC)] + [("k", 0)]
    order += [("x", c) for c in range(FC)] + [("q", 0), ("k", 1)]

    def unit(self, kind, c):
        return self.order.index((kind, c))

    split = unit

    def bank(self, kind, c):
        return self.unit(kind, c) % 2


PRE_UNITS = len(Before.order)
FIRST, COLD, LAST = Pass(0, "first"), Pass(1, "cold"), Pass(B, "last")
UNITS_BEFORE = [PRE_UNITS, PRE_UNITS + FIRST.units, PRE_UNITS + FIRST.units + COLD.units]
SPLITS_BEFORE = [PRE_UNITS, PRE_UNITS + FIRST.splits, PRE_UNITS + FIRST.splits + COLD.splits]
END_UNITS = UNITS_BEFORE[2] + len(PLAN) * (B - 2) + LAST.units
END_SPLITS = SPLITS_BEFORE[2] + (len(PLAN) - TC) * (B - 2) + LAST.splits
TILE_UNITS = HC + FC
assert len({n % 2 for n in UNITS_BEFORE}) == 1 and END_UNITS % 2 == 0 and len(PLAN) % 2 == 0


def xattn_program(nc, x, ctx, l0wq, l0wk, l0wv, wq, wk, wv, wo, w1, w2, cols, bproj, b2, ident, out):
    x2 = nc.dram_tensor("x2_scratch", (B, T, D), F32, kind="Internal").ap()

    place = [-(-nc.sbuf_base // 64) * 64]

    def sb(name, shape, dt, at=None):
        size = 4 * int(np.prod(shape[1:]))
        if at is None:
            at = place[0]
            place[0] += -(-size // 64) * 64
        return nc.alloc_sbuf_tensor_at(name, shape, dt, offset=at)

    weights_at = place[0]
    wq_s = sb("wq_s", [P, 2, FC, D], F32R)
    wk_s = sb("wk_s", [P, 2, FC, D], F32R)
    wv_s = sb("wv_s", [P, 2, FC, D], F32R)
    wo_s = sb("wo_s", [P, 2, FC, D], F32R)
    w2_at = place[0]
    yT = sb("yT", [P, 2, FC, T], F32R)
    q_hl = sb("q_hl", [P, 2, T], F32R)
    k_hl = sb("k_hl", [P, 2, 2, T], F32R)
    q_st = sb("q_st", [P, G, T], F32R)
    k_st = sb("k_st", [P, G, T], F32R)
    v_s = sb("v_s", [P, TC, NH, VW], F32R)
    oT = sb("oT", [P, 2, FC, T], F32R)
    xT = sb("xT", [P, 2, FC, T], F32R)
    p_hi = sb("p_hi", [P, TC, T], F32R)
    p_lo = sb("p_lo", [P, TC, T], F32R)
    tgt2 = sb("tgt2", [P, TC, D], F32)
    xres = sb("xres", [P, TC, D], F32)
    yt = sb("yt", [P, TC, D], F32)
    xt = sb("xt", [P, TC, D], F32)
    scr_at = place[0]
    o_ab = sb("o_ab", [P, 2, T], F32)
    o_a, o_b = o_ab[:, 0], o_ab[:, 1]
    rs = sb("rs", [P, T], F32)
    rs_t = sb("rs_t", [P, T], F32)
    scr = sb("scr", [P, TC, D], F32, at=scr_at)
    o_raw = sb("o_raw", [P, 2, T], F32)
    bp_s = sb("bp_s", [P, D], F32)
    b2_s = sb("b2_s", [P, D], F32)
    id_s = sb("id_s", [P, P], F32)
    id_r = sb("id_r", [P, P], F32R)
    col_s = sb("col_s", [P, NCOLS], F32)
    negmax = sb("negmax", [P, 2, TC], F32R)
    rinv = sb("rinv", [P, T // DK], F32)
    stats = sb("stats", [P, TC, 6], F32)
    mv = sb("mv", [P, TC, 2], F32)
    var_e = sb("var_e", [P, TC], F32)
    rstd = sb("rstd", [P, TC], F32)
    m_half = sb("m_half", [P, TC], F32)
    eps_s = sb("eps_s", [P, TC], F32)
    assert place[0] <= nc.sbuf_usable_end, (place[0], nc.sbuf_usable_end)
    w1_hi = sb("w1_hi", [P, FC, FC, D], F32R, at=weights_at)
    w1_lo = sb("w1_lo", [P, FC, FC, D], F32R, at=weights_at + 4 * FC * FC * D)
    w2_hi = sb("w2_hi", [P, HC, D], F32R, at=w2_at)
    w2_lo = sb("w2_lo", [P, HC, D], F32R, at=w2_at + 4 * HC * D)

    def col(k, c):
        return col_s[:, FC * k + c:FC * k + c + 1]

    GQ, BQ, GKV, BKV, GM, BM = range(6)

    ps_s = nc.alloc_psum_tensor("ps_s", [P, 2, T], F32)
    ps_t = nc.alloc_psum_tensor("ps_t", [P, 2, T], F32)
    ps_o = nc.alloc_psum_tensor("ps_o", [P, T], F32)
    ps_m = nc.alloc_psum_tensor("ps_m", [P, T], F32)
    ps_d = nc.alloc_psum_tensor("ps_d", [P, 2, T], F32)
    out_banks = [ps_s[:, 0], ps_s[:, 1], ps_t[:, 0], ps_t[:, 1]]

    sem = nc.alloc_semaphore
    y_loaded = sem("y_loaded")
    x_loaded = sem("x_loaded")
    res_loaded = sem("res_loaded")
    raw_loaded = {k: sem(f"raw_{k}_loaded") for k in ("xt", "xres", "tgt2", "scr")}
    const_loaded = sem("const_loaded")
    w_hi = sem("w_hi")
    w_split = sem("w_split")
    unit_ready = sem("unit_ready")
    hi_ready = sem("hi_ready")
    split = {k: sem(f"{k}_split") for k in "xyqkvhg"}
    out_done = sem("out_done")
    x_summed = sem("x_summed")
    res_summed = sem("res_summed")
    ln_var = sem("ln_var")
    ln_eps = sem("ln_eps")
    ln_rstd = sem("ln_rstd")
    normed = sem("normed")
    stack_loaded = [sem(f"stack_loaded_{j}") for j in range(G)]
    s_ready = sem("s_ready")
    s_maxed = sem("s_maxed")
    m_spread = sem("m_spread")
    m_moved = sem("m_moved")
    t_ready = sem("t_ready")
    p_exp = sem("p_exp")
    p_split = sem("p_split")
    pv_done = sem("pv_done")
    o_moved = sem("o_moved")
    o_placed = [sem(f"o_placed_{j}") for j in range(G)]
    inv_own = sem("inv_own")
    inv_copied = sem("inv_copied")
    res_own = sem("res_own")
    half_set = sem("half_set")
    inv_ready = sem("inv_ready")
    join_own = sem("join_own")
    o_joined = sem("o_joined")
    consts_set = sem("consts_set")
    ident_set = sem("ident_set")
    stored = sem("stored")
    out_stored = sem("out_stored")
    y2_done = sem("y2_done")

    def rows(dram, b):
        if isinstance(b, int):
            return dram[b].rearrange("(c p) d -> p c d", p=P)
        return dram[bass.ds(b, 1)].rearrange("a (c p) d -> p (a c) d", p=P)

    pieces = ["l0wk", "l0wv", "l0wq", "wv", "wo", "wk", "wq", "w1_0", "w1_1"]
    pieces += ["w2_0", "w1_2", "w2_1", "w1_3", "w2_2", "w2_3"]
    piece_no = {name: n for n, name in enumerate(pieces)}
    raw_in = {"l0wk": ("tgt2", 1), "l0wv": ("xres", 1), "l0wq": ("scr", 1), "wv": ("xres", 2),
              "wo": ("xres", 3), "wk": ("tgt2", 2), "wq": ("xt", 1), "w1_0": ("xt", 2),
              "w1_1": ("tgt2", 3), "w2_0": ("scr", 2), "w1_2": ("xt", 3), "w2_1": ("tgt2", 4),
              "w1_3": ("scr", 3), "w2_2": ("xt", 4), "w2_3": ("tgt2", 5)}
    raw_buf = {"tgt2": tgt2, "xres": xres, "scr": scr, "xt": xt}
    parts = {"l0wk": wk_s, "l0wv": wv_s, "l0wq": wq_s, "wv": wv_s, "wo": wo_s, "wq": wq_s, "wk": wk_s}
    raw_dram = {"l0wk": l0wk, "l0wv": l0wv, "l0wq": l0wq, "wv": wv, "wo": wo, "wq": wq, "wk": wk}
    for j in range(FC):
        raw_dram[f"w1_{j}"] = w1[j]
        raw_dram[f"w2_{j}"] = w2[:, FC * j:FC * j + FC]

    def hi_of(name):
        if name in parts:
            return parts[name][:, 0]
        j = int(name[-1])
        return w1_hi[:, j] if name[1] == "1" else w2_hi[:, FC * j:FC * j + FC]

    def lo_of(name):
        if name in parts:
            return parts[name][:, 1]
        j = int(name[-1])
        return w1_lo[:, j] if name[1] == "1" else w2_lo[:, FC * j:FC * j + FC]

    block_cm = nc.Block()
    block = block_cm.__enter__()

    @block.sync
    def _(sp):
        def load_raw(name):
            buf, _ = raw_in[name]
            sp.dma_start(raw_buf[buf][:], raw_dram[name]).then_inc(raw_loaded[buf], 16)

        def load_stack(p, h):
            g, j = divmod(h, G)
            q, k = slice(j * DK, j * DK + DK), h % G
            through, projected = p.chunk((h - G) * TC + TC), p.n * G + (g + 1)
            if j == 0 and h >= G and not isinstance(p.n, int):
                through, projected = sp.to_reg(through), sp.to_reg(projected)
            if not (p.first and h < G):
                sp.wait_ge(t_ready, through)
            if j == 0:
                sp.wait_ge(split["q"], projected)
            k_hi = k_hl[q, g % 2, 0].unsqueeze(1).broadcast_to([DK, 2, T])
            for dst, src in ((q_st[0:2 * DK, k], q_hl[q]), (k_st[0:2 * DK, k], k_hi),
                             (q_st[2 * DK:KQ, k], q_hl[q, 0]), (k_st[2 * DK:KQ, k], k_hl[q, g % 2, 1])):
                sp.dma_start(dst.bitcast(F32), src.bitcast(F32)).then_inc(stack_loaded[k], 16)

        def place_head(p, h):
            g, j = divmod(h, G)
            q = slice(j * DK, j * DK + DK)
            moved, joined = p.head(h + 1), p.n * G + g if g >= 0 else p.n * G - 1
            if not isinstance(p.n, int):
                moved, joined = sp.to_reg(moved), sp.to_reg(joined)
            sp.wait_ge(o_moved, moved)
            if not (p.first and g == 0):
                sp.wait_ge(o_joined, joined)
            if p.first and h == 0:
                sp.wait_ge(consts_set, 4)
                sp.wait_ge(w_split, 3)
            sp.dma_start(o_ab[q], o_raw[0:2 * DK, h % 2]).then_inc(o_placed[j], 16)
            sp.dma_start(rs[q.start:q.start + 1], o_raw[2 * DK:2 * DK + 1, h % 2]).then_inc(o_placed[j], 16)

        def attend(p):
            for k in range(p.quarters):
                h = (k - (MOVE_AT + 1)) // TC
                late = 3 if h % G == 0 else 0
                if k % TC == late and p.runs(h * TC):
                    place_head(p, h)
                if (k + STACK_AHEAD) % TC == 0:
                    h = (k + STACK_AHEAD) // TC
                    if h < NH or not (p.first or p.last) and h < NH + 2:
                        load_stack(p, h)
                if p.first:
                    if k == 0:
                        sp.wait_ge(w_split, 2)
                        load_raw("wv")
                        load_raw("wk")
                        sp.wait_ge(split["x"], FC)
                        load_raw("wq")
                    if k == 6:
                        sp.wait_ge(w_split, piece_no["wv"] + 1)
                        load_raw("wo")
                    if k == 60:
                        sp.wait_ge(w_split, piece_no["wq"] + 1)
                        sp.dma_start(xt[:], rows(x, 0)).then_inc(x_loaded, 16)
                    continue
                if k == 1:
                    if not p.last:
                        sp.wait_ge(split["y"], (p.n + 1) * FC)
                        sp.dma_start(yt[:], rows(ctx, p.n)).then_inc(y_loaded, 16)
                        sp.wait_ge(split["x"], (p.n + 1) * FC)
                        sp.dma_start(xt[:], rows(x, p.n)).then_inc(x_loaded, 16)
                    else:
                        sp.wait_ge(split["y"], (B + 1) * FC)
                        sp.wait_ge(stored, 16)
                        sp.dma_start(yt[:], rows(x2, 0)).then_inc(x_loaded, 16)
                        sp.wait_ge(split["x"], (B + 1) * FC)
                        load_raw("w1_0")
                if k == 30:
                    if p.follows:
                        sp.wait_ge(out_done, p.n * TC)
                        sp.dma_start(rows(x2, p.n - 2), xres[:]).then_inc(stored, 16)
                if k == 33:
                    if p.follows:
                        sp.wait_ge(stored, (p.n - 1) * 16)
                    else:
                        sp.wait_ge(out_done, TC)
                    sp.dma_start(xres[:], rows(x, p.n - 1)).then_inc(res_loaded, 16)
                if k == 50 and p.last:
                    sp.wait_ge(res_summed, B)
                    load_raw("w1_1")

        sp.dma_start(yt[:], rows(ctx, 0)).then_inc(y_loaded, 16)
        sp.dma_start(id_s[:], ident).then_inc(const_loaded, 16)
        load_raw("l0wk")
        sp.dma_start(col_s[:], cols).then_inc(const_loaded, 16)
        load_raw("l0wv")
        sp.dma_start(xt[:], rows(x, 0)).then_inc(x_loaded, 16)
        load_raw("l0wq")
        sp.dma_start(bp_s[:], bproj.partition_broadcast(P)).then_inc(const_loaded, 16)
        sp.dma_start(b2_s[:], b2.partition_broadcast(P)).then_inc(const_loaded, 16)
        load_stack(FIRST, 0)
        load_stack(FIRST, 1)
        attend(FIRST)
        load_stack(FIRST, NH)
        load_stack(FIRST, NH + 1)
        attend(COLD)
        with sp.Fori(2, B) as i:
            attend(Pass(i))
        attend(LAST)
        sp.wait_ge(o_joined, (B + 1) * G)
        load_raw("w2_0")
        sp.wait_ge(w_split, piece_no["w1_0"] + 1)
        load_raw("w1_2")
        sp.wait_ge(w_split, piece_no["w1_1"] + 1)
        load_raw("w2_1")
        sp.wait_ge(out_done, (B + 1) * TC)
        sp.dma_start(rows(x2, B - 1), xres[:]).then_inc(stored, 16)
        sp.wait_ge(stored, 16 * B)
        sp.dma_start(xres[:], rows(x2, 0)).then_inc(res_loaded, 16)
        sp.dma_start(yt[:], rows(x2, 1)).then_inc(x_loaded, 16)
        for name, before in (("w1_3", "w2_0"), ("w2_2", "w1_2"), ("w2_3", "w2_1")):
            sp.wait_ge(w_split, piece_no[before] + 1)
            load_raw(name)

        def store_tile(t):
            sp.wait_ge(out_done, t * TC + (B + 2) * TC)
            sp.dma_start(rows(out, t), xres[:]).then_inc(out_stored, 16)

        def load_tile(t, final):
            sp.wait_ge(out_stored, t * 16)
            sp.dma_start(xres[:], rows(x2, t)).then_inc(res_loaded, 16)
            if not final:
                sp.wait_ge(unit_ready, t * TILE_UNITS + END_UNITS)
                sp.dma_start(yt[:], rows(x2, t + 1)).then_inc(x_loaded, 16)

        store_tile(0)
        with sp.Fori(1, B - 1) as i:
            load_tile(i, False)
            store_tile(i)
        load_tile(B - 1, True)
        store_tile(B - 1)
        sp.wait_ge(out_stored, 16 * B)

    @block.tensor
    def _(pe):
        taken = {0: [], 1: []}

        def bank(p, kind, c):
            b = p.bank(kind, c)
            for s, value in taken[b]:
                pe.wait_ge(s, value)
            return ps_d[:, b]

        def filled(ins, p, kind, c, s, value):
            ins.then_inc(unit_ready, 1)
            taken[p.bank(kind, c)] = [(s, value)]

        def transposes(p, kind, c, src, k):
            dst = bank(p, kind, c)
            for t in range(TC):
                ins = nc.tensor.transpose(dst[:, t * P:t * P + P], src[:, t, c * P:c * P + P], id_s[:])
            filled(ins, p, kind, c, split[kind], k + (c + 1))

        def products(dst, lhs, rhs, chunks):
            for c in range(chunks):
                for n, (a, b) in enumerate(((0, 0), (0, 1), (1, 0))):
                    ins = nc.tensor.matmul(dst, lhs(a, c), rhs(b, c), start=(c == 0 and n == 0),
                                           stop=(c == chunks - 1 and n == 2))
            return ins

        def part(p, kind, c, i):
            if kind in "xyh":
                if c == 0:
                    n = {"x": p.n * 2 + 2, "y": p.n * 2 + 1, "h": 2 * B + 1}[kind]
                    pe.wait_ge(normed, n)
                transposes(p, kind, c, xt if kind == "x" else yt, 0 if kind == "h" else (p.n + 1) * FC)
                return
            if kind in "qk":
                w, src, value = (wq_s, xT, p.n * G + (c + 1)) if kind == "q" else (wk_s, yT, p.n * G + (c + 1))
                lhs = [w[:, a, i, (c % G) * P:(c % G) * P + P] for a in range(2)]
                rhs = [src[:, b, i] for b in range(2)]
                if c == G and i == 0:
                    pe.wait_ge(split["x" if kind == "q" else "y"], (p.n + 2) * FC)
                    if p.first:
                        pe.wait_ge(w_split, piece_no["w" + kind] + 1)
            elif kind == "v":
                value = p.n * TC + (c + 1)
                lhs = [yT[:, a, i, c * P:c * P + P] for a in range(2)]
                rhs = [wv_s[:, b, i] for b in range(2)]
            else:
                n = p.n + 1 if kind == "end" else p.n
                value = (n - 1) * TC + (c + 1)
                lhs = [oT[:, a, i, c * P:c * P + P] for a in range(2)]
                rhs = [wo_s[:, b, i] for b in range(2)]
                if c == 0 and i == 0:
                    pe.wait_ge(o_joined, n * G)
            dst = bank(p, kind, c) if i == 0 else ps_d[:, p.bank(kind, c)]
            for n, (a, b) in enumerate(((0, 0), (0, 1), (1, 0))):
                ins = nc.tensor.matmul(dst, lhs[a], rhs[b], start=(i == 0 and n == 0),
                                       stop=(i == FC - 1 and n == 2))
            if i == FC - 1:
                filled(ins, p, kind, c, out_done if kind in ("out", "end") else split[kind], value)

        def attend(p):
            busy = [(split["q"], p.n * G + 1), (split["k"], p.n * G + 2), (split["x"], (p.n + 1) * FC)]
            taken[0], taken[1] = list(busy), list(busy)
            for k in range(p.quarters):
                if k < CH:
                    h, c = divmod(k, TC)
                    if c == 0:
                        pe.wait_ge(stack_loaded[h % G], (p.n * G + (h // G + 1)) * (16 * STACK_DMAS))
                    if not (p.first and k < 2):
                        pe.wait_ge(s_maxed, p.chunk(k - 1))
                    nc.tensor.matmul(ps_s[:, c % 2], q_st[0:KQ, h % G, c * P:c * P + P],
                                     k_st[0:KQ, h % G], start=True, stop=True).then_inc(s_ready, 1)
                j = k - SHIFT_LAG
                if p.runs(j):
                    h, c = divmod(j, TC)
                    if c == 0:
                        pe.wait_ge(m_moved, p.head(h + 1))
                        if p.first and h == 0:
                            pe.wait_ge(consts_set, 1)
                    if not (p.first and j < 2):
                        pe.wait_ge(p_split, p.chunk(j - 1))
                    nc.tensor.matmul(ps_t[:, c % 2], k_st[0:KM, h % G, c * P:c * P + P],
                                     q_st[0:KM, h % G], start=True, stop=True).then_inc(t_ready, 1)
                for kind, c, i in p.parts.get(k, []):
                    part(p, kind, c, i)
                j = k - WEIGH_LAG
                if p.runs(j):
                    h, c = divmod(j, TC)
                    if c == 0 and not (p.first and h == 0):
                        pe.wait_ge(o_moved, p.head(h))
                    if h == 0:
                        pe.wait_ge(split["v"], p.n * TC + (c + 1))
                        if p.first:
                            pe.wait_ge(consts_set, 2)
                    pe.wait_ge(p_split, p.chunk(j + 1))
                    for n, src in enumerate((p_hi, p_lo)):
                        ins = nc.tensor.matmul(ps_o[0:VW], v_s[:, c, h % NH], src[:, c],
                                               start=(c == 0 and n == 0), stop=(c == TC - 1 and n == 1))
                    ins.then_inc(pv_done, 1)
                if (k - SPREAD_AT) % TC == 0 and p.runs(k - SPREAD_AT):
                    h = (k - SPREAD_AT) // TC
                    pe.wait_ge(s_maxed, p.chunk(h * TC + TC))
                    if not (p.first and h == 0):
                        pe.wait_ge(m_moved, p.head(h))
                    else:
                        pe.wait_ge(ident_set, 1)
                    for c in range(TC):
                        ins = nc.tensor.matmul(ps_m[:, c * P:c * P + P],
                                               negmax[:, h % 2, c:c + 1].broadcast_to([P, P]),
                                               id_r[:], start=True, stop=True)
                    ins.then_inc(m_spread, 1)

        pre = Before()
        pe.wait_ge(y_loaded, 16)
        pe.wait_ge(const_loaded, 64)
        for c in range(FC):
            transposes(pre, "y", c, yt, 0)
        pe.wait_ge(split["y"], FC)
        pe.wait_ge(w_split, 2)
        for c in range(TC):
            for i in range(FC):
                part(pre, "v", c, i)
        for i in range(FC):
            part(pre, "k", 0, i)
        pe.wait_ge(x_loaded, 16)
        for c in range(FC):
            transposes(pre, "x", c, xt, 0)
        pe.wait_ge(split["x"], FC)
        pe.wait_ge(w_split, 3)
        for i in range(FC):
            part(pre, "q", 0, i)
        for i in range(FC):
            part(pre, "k", 1, i)

        attend(FIRST)
        for c in range(TC):
            dst = bank(FIRST, "v", c)
            ins = products(dst, lambda a, i: yT[:, a, i, c * P:c * P + P], lambda b, i: wv_s[:, b, i], FC)
            filled(ins, FIRST, "v", c, split["v"], TC + c + 1)
        pe.wait_ge(o_joined, G)
        for t in range(TC):
            dst = bank(FIRST, "out", t)
            for c in range(FC):
                ins = nc.tensor.transpose(dst[:, c * P:c * P + P], xres[:, c, t * P:t * P + P], id_s[:])
            filled(ins, FIRST, "out", t, out_done, t + 1)
        pe.wait_ge(normed, 2)
        for c in range(FC):
            transposes(FIRST, "x", c, xt, FC)
        for i in range(FC):
            part(FIRST, "q", G, i)
        attend(COLD)
        with pe.Fori(2, B) as i:
            attend(Pass(i))
        attend(LAST)
        for c in range(TC):
            for i in range(FC):
                part(LAST, "end", c, i)

        def hidden(t, c):
            b = c % 2
            if c == 0:
                pe.wait_ge(split["h"], (t + 1) * FC)
                if isinstance(t, int) and t == 0:
                    pe.wait_ge(out_done, (B + 1) * TC)
            if c >= 2:
                pe.wait_ge(split["g"], t * HC + (c - 1))
            if isinstance(t, int) and t == 0 and c % FC == 0:
                pe.wait_ge(w_split, piece_no[f"w1_{c // FC}"] + 1)
            q, j = divmod(c, FC)
            w = (w1_hi, w1_lo)
            ins = products(ps_d[:, b], lambda a, k: w[a][:, q, k, j * P:j * P + P],
                           lambda b, k: xT[:, b, k], FC)
            ins.then_inc(unit_ready, 1)

        def output(t, c):
            if c == 0 and not (isinstance(t, int) and t == 0):
                pe.wait_ge(out_done, (t + (B + 1)) * TC)
            if isinstance(t, int) and t == 0 and c % FC == 0:
                pe.wait_ge(w_split, piece_no[f"w2_{c // FC}"] + 1)
            pe.wait_ge(split["g"], t * HC + (c + 1))
            g, w = (p_hi, p_lo), (w2_hi, w2_lo)
            for k in range(TC):
                for n, (a, b) in enumerate(((0, 0), (0, 1), (1, 0))):
                    ins = nc.tensor.matmul(out_banks[k], g[a][:, c % TC, k * P:k * P + P], w[b][:, c],
                                           start=(c == 0 and n == 0), stop=(c == HC - 1 and n == 2))
            ins.then_inc(y2_done, 1)

        def tile(t, final):
            for c in range(HC):
                hidden(t, c)
                if c == HC - 1 and not final:
                    pe.wait_ge(normed, t + (2 * B + 2))
                    for k in range(FC):
                        if k < 2:
                            pe.wait_ge(split["g"], t * HC + (HC - 1 + k))
                        else:
                            pe.wait_ge(split["h"], t * FC + (FC + k - 1))
                        for r in range(TC):
                            ins = nc.tensor.transpose(ps_d[:, k % 2, r * P:r * P + P],
                                                      yt[:, r, k * P:k * P + P], id_s[:])
                        ins.then_inc(unit_ready, 1)
                if c >= 1:
                    output(t, c - 1)
            output(t, HC - 1)

        tile(0, False)
        with pe.Fori(1, B - 1) as i:
            tile(i, False)
        tile(B - 1, True)

    @block.scalar
    def _(act):
        def hi_weights(name):
            buf, use = raw_in[name]
            act.wait_ge(raw_loaded[buf], 16 * use)
            act.activation(hi_of(name), raw_buf[buf][:], ACT.Identity).then_inc(w_hi, 1)

        def hi_plain(p, kind, c, dst, src):
            act.wait_ge(unit_ready, p.unit(kind, c) + 1)
            act.activation(dst, src, ACT.Identity).then_inc(hi_ready, 1)

        def hi_affine(p, kind, c, dst, gain, bias):
            act.wait_ge(unit_ready, p.unit(kind, c) + 1)
            b = ps_d[:, p.bank(kind, c)]
            act.activation(dst, b, ACT.Identity, bias=col(bias, c), scale=col(gain, c))
            act.activation(b, b, ACT.Identity, bias=col(bias, c), scale=col(gain, c)).then_inc(hi_ready, 1)

        def hi(p, kind, c):
            if kind in "xyh":
                gain, bias = {"x": (GQ, BQ), "y": (GKV, BKV), "h": (GM, BM)}[kind]
                hi_affine(p, kind, c, (yT if kind == "y" else xT)[:, 0, c], gain, bias)
            elif kind == "v":
                if p.follows:
                    act.wait_ge(pv_done, p.chunk(c + 1 - TC))
                hi_value(p, c)
            else:
                groups = p.n * G + (c if kind == "q" else c - 1)
                if not (p.first and c <= (0 if kind == "q" else 1)):
                    for j in range(G):
                        act.wait_ge(stack_loaded[j], groups * (16 * STACK_DMAS))
                dst = q_hl[:, 0] if kind == "q" else k_hl[:, c % 2, 0]
                hi_plain(p, kind, c, dst, ps_d[:, p.bank(kind, c)])

        def hi_value(p, c):
            hi_plain(p, "v", c, v_s[:, c, :, 0:2 * DK:2],
                     ps_d[:, p.bank("v", c)].rearrange("p (h d) -> p h d", h=NH))

        def attend(p):
            for k in range(p.quarters):
                if (k - MAXIMA_AT) % TC == 0 and p.runs(k - MAXIMA_AT):
                    h = (k - MAXIMA_AT) // TC
                    act.wait_ge(m_spread, p.head(h + 1))
                    act.activation(q_st[KQ:KM, h % G], ps_m[KQ:KM], ACT.Identity).then_inc(m_moved, 1)
                j = k - SHIFT_LAG
                if p.runs(j):
                    c = j % TC
                    act.wait_ge(t_ready, p.chunk(j + 1))
                    if not (p.first and j < TC):
                        act.wait_ge(pv_done, p.chunk(j + 1 - TC))
                    act.activation(p_hi[:, c], ps_t[:, c % 2], ACT.Exp, scale=SCALE)
                    act.activation(ps_t[:, c % 2], ps_t[:, c % 2], ACT.Exp, scale=SCALE).then_inc(p_exp, 1)
                if (k - MOVE_AT) % TC == 0 and p.runs(k - MOVE_AT):
                    h = (k - MOVE_AT) // TC
                    act.wait_ge(pv_done, p.chunk(h * TC + TC))
                    if not (p.first and h < 2):
                        g = (h - 2) // G
                        placed = p.n * G + (g + 1) if g >= -1 else p.n * G - 1
                        act.wait_ge(o_placed[(h - 2) % G], placed * (16 * PLACE_DMAS))
                    act.activation(o_raw[0:VW, h % 2], ps_o[0:VW], ACT.Identity).then_inc(o_moved, 1)
                for kind, c in p.his.get(k, []):
                    hi(p, kind, c)
                if p.first:
                    if k == 2:
                        act.wait_ge(split["v"], TC)
                        hi_weights("wv")
                    if k == 8:
                        hi_weights("wo")
                    if k == 32:
                        act.wait_ge(unit_ready, p.unit("k", 3) + 1)
                        hi_weights("wk")
                    if k == 40:
                        act.wait_ge(unit_ready, p.unit("q", 3) + 1)
                        hi_weights("wq")
                if p.last:
                    if k == 46:
                        hi_weights("w1_0")
                    if k == 60:
                        hi_weights("w1_1")

        pre = Before()
        act.wait_ge(const_loaded, 64)
        act.activation(id_r[:], id_s[:], ACT.Identity).then_inc(ident_set, 1)
        for name in ("l0wk", "l0wv", "l0wq"):
            hi_weights(name)
        for c in range(FC):
            hi_plain(pre, "y", c, yT[:, 0, c], ps_d[:, pre.bank("y", c)])
        for c in range(TC):
            hi_value(pre, c)
        hi(pre, "k", 0)
        for c in range(FC):
            hi_plain(pre, "x", c, xT[:, 0, c], ps_d[:, pre.bank("x", c)])
        hi(pre, "q", 0)
        hi(pre, "k", 1)
        attend(FIRST)
        for c in range(TC):
            hi_value(FIRST, c)
        for c in range(FC):
            hi(FIRST, "x", c)
        hi(FIRST, "q", G)
        attend(COLD)
        with act.Fori(2, B) as i:
            attend(Pass(i))
        attend(LAST)

        def tile(t, final):
            for c in range(HC):
                if isinstance(t, int) and t == 0 and c in (0, 1, 4, 6, 8, 10):
                    name = {0: "w2_0", 1: "w1_2", 4: "w2_1", 6: "w1_3", 8: "w2_2", 10: "w2_3"}[c]
                    if c == 0:
                        act.wait_ge(unit_ready, END_UNITS)
                    hi_weights(name)
                act.wait_ge(unit_ready, t * TILE_UNITS + (END_UNITS + c + 1))
                if not (isinstance(t, int) and t == 0 and c < TC):
                    act.wait_ge(y2_done, t * HC + (c - TC + 1))
                else:
                    act.wait_ge(pv_done, (B + 1) * CH)
                b1 = col_s[:, 6 * FC + c:6 * FC + c + 1]
                act.activation(p_hi[:, c % TC], ps_d[:, c % 2], ACT.Gelu, bias=b1)
                act.activation(ps_d[:, c % 2], ps_d[:, c % 2], ACT.Gelu, bias=b1).then_inc(hi_ready, 1)
            if not final:
                for k in range(FC):
                    act.wait_ge(unit_ready, t * TILE_UNITS + (END_UNITS + HC + k + 1))
                    b = ps_d[:, k % 2]
                    act.activation(xT[:, 0, k], b, ACT.Identity, bias=col(BM, k), scale=col(GM, k))
                    act.activation(b, b, ACT.Identity, bias=col(BM, k), scale=col(GM, k)).then_inc(hi_ready, 1)

        tile(0, False)
        with act.Fori(1, B - 1) as i:
            tile(i, False)
        tile(B - 1, True)

    @block.vector
    def _(dve):
        def lo(p, kind, c, dst, src, hi):
            dve.wait_ge(hi_ready, p.split(kind, c) + 1)
            dve.tensor_tensor(dst, src, hi, ALU.subtract).then_inc(split[kind], 1)

        def lo_unit(p, kind, c):
            b = ps_d[:, p.bank(kind, c)]
            if kind in "xyh":
                dst = yT if kind == "y" else xT
                lo(p, kind, c, dst[:, 1, c], b, dst[:, 0, c].bitcast(F32))
            elif kind == "v":
                lo(p, "v", c, v_s[:, c, :, 1:2 * DK:2], b.rearrange("p (h d) -> p h d", h=NH),
                   v_s[:, c, :, 0:2 * DK:2].bitcast(F32))
            elif kind == "q":
                lo(p, kind, c, q_hl[:, 1], b, q_hl[:, 0].bitcast(F32))
            else:
                lo(p, kind, c, k_hl[:, c % 2, 1], b, k_hl[:, c % 2, 0].bitcast(F32))

        def norm_stats(rows_in):
            for t in range(TC):
                dve.bn_stats(stats[:, t], rows_in[:, t])
            norm_aggregate()

        def norm_aggregate():
            dve.drain()
            for t in range(TC):
                ins = dve.bn_aggr(mv[:, t], stats[:, t])
            ins.then_inc(ln_var, 1)

        def norm_apply(rows_in, t, n):
            if t == 0:
                dve.wait_ge(ln_rstd, n + 1)
            ins = dve.tensor_scalar(rows_in[:, t], rows_in[:, t], mv[:, t, 0:1], rstd[:, t:t + 1],
                                    ALU.subtract, ALU.mult)
            if t == TC - 1:
                ins.then_inc(normed, 1)

        def invert(p, g, step):
            done = p.n * G + g if g >= 0 else p.n * G - 1
            if step == 0:
                for j in range(G):
                    dve.wait_ge(o_placed[j], (done + 1) * (16 * PLACE_DMAS))
                dve.transpose(rs_t[:], rs[:]).then_inc(inv_own, 1)
            elif step == 1:
                dve.wait_ge(inv_own, done * 2 + 1)
                sums = rs_t[:].rearrange("p (b e) -> p b e", e=DK)[:, :, 0]
                dve.reciprocal(rinv[:], sums).then_inc(inv_own, 1)
            elif step == 2:
                dve.wait_ge(inv_own, done * 2 + 2)
                dve.tensor_copy(rs_t[:].rearrange("p (b e) -> p b e", e=DK),
                                rinv[:].unsqueeze(2).broadcast_to([P, T // DK, DK])).then_inc(inv_copied, 1)
            else:
                dve.wait_ge(inv_copied, done + 1)
                dve.transpose(rs[:], rs_t[:]).then_inc(inv_ready, 1)

        def residual(p, kind, t):
            if t == 0:
                dve.wait_ge(res_summed, B if kind == "end" else p.n - 1)
            dve.wait_ge(unit_ready, p.unit(kind, t) + 1)
            dve.tensor_tensor(xres[:, t], ps_d[:, p.bank(kind, t)], xres[:, t], ALU.add)\
               .then_inc(out_done, 1)

        def attend(p):
            for k in range(p.quarters):
                if p.runs(k - 1):
                    h, c = divmod(k - 1, TC)
                    dve.wait_ge(s_ready, p.chunk(k))
                    if c == 0 and not (p.first and h < 2):
                        dve.wait_ge(m_spread, p.head(h - 1))
                    dve.tensor_reduce(negmax[:, h % 2, c:c + 1], ps_s[:, c % 2], AX.X, ALU.max,
                                      negate=True).then_inc(s_maxed, 1)
                j = k - (SHIFT_LAG + 1)
                if p.runs(j):
                    c = j % TC
                    dve.wait_ge(p_exp, p.chunk(j + 1))
                    dve.tensor_tensor(p_lo[:, c], ps_t[:, c % 2], p_hi[:, c].bitcast(F32),
                                      ALU.subtract).then_inc(p_split, 1)
                for kind, c in p.los.get(k, []):
                    if kind == "out":
                        residual(p, kind, c)
                    else:
                        lo_unit(p, kind, c)
                g, step = divmod(k - INVERT_AT, TC * G)
                if step < 4 and p.runs(g * TC * G) and not (p.first and g == G - 1):
                    invert(p, g, step)
                if 4 <= k < 8:
                    if k == 4 and p.last:
                        dve.wait_ge(x_loaded, (B + 2) * 16)
                    elif k == 4 and not p.first:
                        dve.wait_ge(y_loaded, (p.n + 1) * 16)
                    dve.bn_stats(stats[:, k - 4], yt[:, k - 4])
                if k == 8:
                    norm_aggregate()
                if 12 <= k < 16:
                    norm_apply(yt, k - 12, p.n * 2)
                if not (p.first or p.last):
                    if 18 <= k < 22:
                        if k == 18:
                            dve.wait_ge(x_summed, p.n + 1)
                        dve.bn_stats(stats[:, k - 18], xt[:, k - 18])
                    if k == 22:
                        norm_aggregate()
                    if 34 <= k < 38:
                        norm_apply(xt, k - 34, p.n * 2 + 1)

        dve.memset(k_st[KQ:KM].bitcast(F32), 1.0).then_inc(consts_set, 1)
        dve.memset(v_s[:, :, :, 2 * DK:VW].bitcast(F32), 1.0).then_inc(consts_set, 1)
        pre = Before()
        for kind, c in pre.order:
            lo_unit(pre, kind, c)
        dve.wait_ge(w_split, 3)
        dve.memset(rs[:], 1.0).then_inc(consts_set, 1)
        dve.memset(rs_t[:], 1.0).then_inc(consts_set, 1)
        attend(FIRST)
        for c in range(TC):
            lo_unit(FIRST, "v", c)
        for step in range(4):
            invert(FIRST, G - 1, step)
        for t in range(TC):
            dve.wait_ge(unit_ready, FIRST.unit("out", t) + 1)
            if t == 0:
                dve.wait_ge(w_split, piece_no["wk"] + 1)
            dve.tensor_copy(tgt2[:, t], ps_d[:, FIRST.bank("out", t)]).then_inc(out_done, 1)
        dve.wait_ge(x_summed, 1)
        norm_stats(xt)
        for t in range(TC):
            norm_apply(xt, t, 1)
        for c in range(FC):
            lo_unit(FIRST, "x", c)
        lo_unit(FIRST, "q", G)
        attend(COLD)
        with dve.Fori(2, B) as i:
            attend(Pass(i))
        attend(LAST)
        for t in range(TC):
            residual(LAST, "end", t)

        def tile(t, final):
            for c in range(HC):
                dve.wait_ge(hi_ready, t * TILE_UNITS + (END_SPLITS + c + 1))
                dve.tensor_tensor(p_lo[:, c % TC], ps_d[:, c % 2], p_hi[:, c % TC].bitcast(F32),
                                  ALU.subtract).then_inc(split["g"], 1)
                if c == 8 and not final:
                    dve.wait_ge(x_loaded, (t + (B + 3)) * 16)
                    norm_stats(yt)
                if c == 9 and not final:
                    for r in range(TC):
                        norm_apply(yt, r, t + (2 * B + 1))
            if not final:
                for k in range(FC):
                    dve.wait_ge(hi_ready, t * TILE_UNITS + (END_SPLITS + HC + k + 1))
                    dve.tensor_tensor(xT[:, 1, k], ps_d[:, k % 2], xT[:, 0, k].bitcast(F32),
                                      ALU.subtract).then_inc(split["h"], 1)
            dve.wait_ge(y2_done, (t + 1) * HC)
            dve.wait_ge(res_summed, t + (B + 1))
            for k in range(TC):
                dve.tensor_tensor(xres[:, k], out_banks[k], xres[:, k], ALU.add).then_inc(out_done, 1)

        tile(0, False)
        with dve.Fori(1, B - 1) as i:
            tile(i, False)
        tile(B - 1, True)

    @block.gpsimd
    def _(pool):
        def lo_weights(name):
            buf, _ = raw_in[name]
            pool.wait_ge(w_hi, piece_no[name] + 1)
            pool.tensor_tensor(lo_of(name), raw_buf[buf][:], hi_of(name).bitcast(F32), ALU.subtract)\
                .then_inc(w_split, 1)

        def norm_rstd(n):
            pool.wait_ge(ln_var, n + 1)
            pool.tensor_tensor(var_e[:], mv[:, :, 1], eps_s[:], ALU.add).then_inc(ln_eps, 1)
            pool.wait_ge(ln_eps, n + 1)
            pool.tensor_tensor(rstd[:], var_e[:], m_half[:], ALU.pow).then_inc(ln_rstd, 1)

        def join(p, g):
            done = p.n * G + g if g >= 0 else p.n * G - 1
            for j in range(G):
                pool.wait_ge(o_placed[j], (done + 1) * (16 * PLACE_DMAS))
            pool.tensor_tensor(o_a, o_a, o_b, ALU.add).then_inc(join_own, 1)
            pool.wait_ge(join_own, done * 3 + 1)
            pool.wait_ge(inv_ready, done + 1)
            if p.first:
                if g == 0:
                    pool.wait_ge(w_split, piece_no["wo"] + 1)
                pool.tensor_tensor(xres[:, g], o_a, rs[:], ALU.mult).then_inc(o_joined, 1)
                pool.sem_inc(join_own, 2)
                return
            if g == 0 and p.follows:
                pool.wait_ge(unit_ready, p.unit("out", TC - 1) + 1)
            g %= G
            pool.tensor_tensor(oT[:, 0, g], o_a, rs[:], ALU.mult).then_inc(join_own, 1)
            pool.tensor_tensor(o_a, o_a, rs[:], ALU.mult).then_inc(join_own, 1)
            pool.wait_ge(join_own, done * 3 + 3)
            pool.tensor_tensor(oT[:, 1, g], o_a, oT[:, 0, g].bitcast(F32), ALU.subtract)                .then_inc(o_joined, 1)

        def attend(p):
            for k in range(p.quarters):
                if k == 2 and not p.first and not p.last:
                    pool.wait_ge(x_loaded, (p.n + 2) * 16)
                    pool.tensor_tensor(xt[:], xt[:], tgt2[:], ALU.add).then_inc(x_summed, 1)
                if k == 8:
                    norm_rstd(p.n * 2)
                if k == 22 and not p.first and not p.last:
                    norm_rstd(p.n * 2 + 1)
                g, step = divmod(k - INVERT_AT, TC * G)
                if step == 0 and p.runs(g * TC * G) and not (p.first and g == G - 1):
                    join(p, g)
                if k == 46 and not p.first:
                    pool.wait_ge(res_loaded, p.n * 16)
                    pool.tensor_tensor(xres[:], xres[:], tgt2[:], ALU.add).then_inc(res_own, 1)
                    pool.wait_ge(res_own, p.n)
                    pool.tensor_tensor(xres[:], xres[:], bp_s[:].unsqueeze(1).broadcast_to([P, TC, D]),
                                       ALU.add).then_inc(res_summed, 1)
                if p.first:
                    if k == 2:
                        lo_weights("wv")
                    if k == 8:
                        lo_weights("wo")
                    if k == 32:
                        lo_weights("wk")
                    if k == 43:
                        lo_weights("wq")
                if p.last:
                    if k == 62:
                        lo_weights("w1_0")
                    if k == 78:
                        lo_weights("w1_1")

        pool.memset(m_half[:], -0.5).then_inc(half_set, 1)
        pool.memset(eps_s[:], EPS).then_inc(half_set, 1)
        pool.wait_ge(half_set, 2)
        for name in ("l0wk", "l0wv", "l0wq"):
            lo_weights(name)
        attend(FIRST)
        join(FIRST, G - 1)
        pool.wait_ge(x_loaded, 32)
        pool.wait_ge(out_done, TC)
        pool.tensor_tensor(xt[:], xt[:], tgt2[:], ALU.add).then_inc(x_summed, 1)
        norm_rstd(1)
        attend(COLD)
        with pool.Fori(2, B) as i:
            attend(Pass(i))
        attend(LAST)

        def add_bias(t):
            pool.wait_ge(res_loaded, (t + (B + 1)) * 16)
            pool.tensor_tensor(xres[:], xres[:], b2_s[:].unsqueeze(1).broadcast_to([P, TC, D]),
                               ALU.add).then_inc(res_summed, 1)

        for name in ("w2_0", "w1_2", "w2_1"):
            lo_weights(name)
        add_bias(0)
        for name in ("w1_3", "w2_2", "w2_3"):
            lo_weights(name)
        norm_rstd(2 * B + 1)
        with pool.Fori(1, B - 1) as i:
            add_bias(i)
            norm_rstd(i + (2 * B + 1))
        add_bias(B - 1)

    block_cm.__exit__(None, None, None)


def kernel(x, ctx_1024, L0_xattn_Wq, L0_xattn_Wk, L0_xattn_Wv, L1_xattn_gq, L1_xattn_bq, L1_xattn_gkv,
           L1_xattn_bkv, L1_xattn_Wq, L1_xattn_Wkv, L1_xattn_Wproj, L1_xattn_bproj, L1_xattn_gm,
           L1_xattn_bm, L1_xattn_W1, L1_xattn_b1, L1_xattn_W2, L1_xattn_b2):
    import concourse.bacc as bacc
    from concourse.bass_utils import run_bass_kernel_spmd

    def chunked(w):
        w = np.asarray(w)
        return np.ascontiguousarray(w.reshape(-1, P, w.shape[1]).transpose(1, 0, 2))

    def columns(v):
        return np.asarray(v).reshape(-1, P).T

    wkv = np.asarray(L1_xattn_Wkv)
    w1 = np.asarray(L1_xattn_W1).reshape(FC, P, FC, D).transpose(2, 1, 0, 3)
    arrays = {
        "x": np.ascontiguousarray(x),
        "ctx": np.ascontiguousarray(ctx_1024),
        "l0wq": chunked(np.asarray(L0_xattn_Wq).T),
        "l0wk": chunked(np.asarray(L0_xattn_Wk).T),
        "l0wv": chunked(np.asarray(L0_xattn_Wv).T),
        "wq": chunked(L1_xattn_Wq),
        "wk": chunked(wkv[:, :D]),
        "wv": chunked(wkv[:, D:]),
        "wo": chunked(L1_xattn_Wproj),
        "w1": np.ascontiguousarray(w1),
        "w2": chunked(L1_xattn_W2),
        "cols": np.ascontiguousarray(np.concatenate(
            [columns(v) for v in (L1_xattn_gq, L1_xattn_bq, L1_xattn_gkv, L1_xattn_bkv, L1_xattn_gm,
                                  L1_xattn_bm, L1_xattn_b1)], axis=1)),
        "bproj": np.ascontiguousarray(L1_xattn_bproj),
        "b2": np.ascontiguousarray(L1_xattn_b2),
        "ident": np.eye(P, dtype=np.float32),
    }
    nc = bacc.Bacc("TRN2", target_bir_lowering=False, num_devices=1, dynamic_dma_scratch_size=1024)
    args = [nc.dram_tensor(name, a.shape, mybir.dt.from_np(a.dtype), kind="ExternalInput").ap()
            for name, a in arrays.items()]
    out = nc.dram_tensor("out", (B, T, D), F32, kind="ExternalOutput").ap()
    xattn_program(nc, *args, out)
    r = run_bass_kernel_spmd(nc, [arrays], core_ids=[0])
    return r.results[0]["out"]
```

```python
import numpy as np

import concourse.bass as bass
from concourse import mybir

F32 = mybir.dt.float32
F32R = mybir.dt.float32r
ACT = mybir.ActivationFunctionType
ALU = mybir.AluOpType
AX = mybir.AxisListType

P = 128
T = 512
D = 512
F = 2048
B = 8
NH = 16
DK = D // NH
FC = D // P
TC = T // P
HC = F // P
G = P // DK
SCALE = float(DK) ** -0.5
EPS = 1e-5

KQ = 3 * DK
KM = KQ + 1
VW = 2 * DK + 1
CH = NH * TC
STACK_DMAS = 4
PLACE_DMAS = 2
NCOLS = 6 * FC + HC

SHIFT_LAG = 6
WEIGH_LAG = 8
SPREAD_AT = TC
MAXIMA_AT = SPREAD_AT + 1
MOVE_AT = TC - 1 + WEIGH_LAG
INVERT_AT = 26
DRAIN = 18
POOL_CHUNK = 2
STACK_AHEAD = 6

EARLY = TC
TURN_AT = 12

PLAN = [
    (("v", 0), 0, (4, 4, 5, 5)), (("v", 1), 1, (5, 6, 6, 6)), (("v", 2), 0, (7, 7, 7, 8)),
    (("v", 3), 1, (8, 8, 9, 9)), (("q", 1), 0, (10, 10, 11, 11)), (("k", 2), 1, (12, 13, 14, 15)),
    (("out", 0), 0, (16, 17, 17, 18)), (("out", 1), 1, (18, 19, 20, 20)), (("q", 2), 0, (21, 22, 23, 23)),
    (("k", 3), 1, (24, 25, 26, 26)), (("out", 2), 0, (26, 27, 27, 28)),
    (("y", 0), 1, (28,)), (("y", 1), 1, (30,)), (("out", 3), 0, (29, 30, 31, 31)), (("y", 2), 1, (32,)),
    (("y", 3), 1, (34,)), (("q", 3), 0, (33, 34, 35, 36)),
    (("x", 0), 1, (37,)), (("x", 1), 1, (39,)), (("x", 2), 1, (41,)),
    (("k", 4), 0, (42, 43, 44, 45)), (("x", 3), 1, (43,)),
    (("q", 4), 1, (50, 51, 52, 53)), (("k", 5), 0, (58, 59, 60, 61)),
]


def plus(a, b):
    return a + b if b >= 0 else a - (-b)


class Pass:

    def __init__(self, n, kind="steady"):
        self.n = n
        self.first, self.cold, self.last = kind == "first", kind == "cold", kind == "last"
        self.follows = kind in ("steady", "last")
        self.quarters = CH + (DRAIN if self.first or self.last else 0)
        if self.first:
            plan = [u for u in PLAN if u[0][0] in "vyqk" and u[0] != ("q", G)]
            after = [("next v", c) for c in range(TC)] + [("out", c) for c in range(TC)]
            after += [("x", c) for c in range(FC)] + [("q", G)]
        elif self.cold:
            plan, after = [u for u in PLAN if u[0][0] not in ("v", "out")], []
        elif self.last:
            plan = [(("h", u[0][1]), *u[1:]) if u[0][0] == "x" else u for u in PLAN
                    if u[0][0] != "y" and not (u[0][0] in "qk" and u[0][1] >= G)]
            after = [("g", c) for c in range(EARLY)] + [("end", c) for c in range(TC)]
        else:
            plan, after = PLAN, []
        self.parts, self.his, self.los, filled_at, hi_at = {}, {}, {}, {}, {}
        for (kind, c), _, quarters in plan:
            for i, k in enumerate(quarters):
                self.parts.setdefault(k, []).append((kind, c, i))
            filled_at[kind, c] = hi = quarters[-1]
            free = {"q": c - 1, "k": c - 2}.get(kind, 0)
            if free > 0:
                hi = max(hi, TC * G * free + SHIFT_LAG + 2)
            hi_at[kind, c] = hi
        order = sorted(filled_at, key=filled_at.get) + after
        split = sorted((u for u in hi_at if u[0] != "out"), key=hi_at.get)
        for kind, c in split:
            self.his.setdefault(hi_at[kind, c], []).append((kind, c))
        for kind, c in sorted(hi_at, key=hi_at.get):
            self.los.setdefault(hi_at[kind, c] + 1, []).append((kind, c))
        split += [u for u in after if u[0] not in ("out", "end")]
        self.no = {u: i for i, u in enumerate(order)}
        self.units, self.splits = len(order), len(split)
        self.split_no = {u: i for i, u in enumerate(split)}
        self.banks = {u: b for u, b, _ in plan}
        self.banks.update({u: i % 2 for i, u in enumerate(after)})

    def base(self, steady, before):
        if isinstance(self.n, int) and self.n < 2:
            return before[self.n]
        return (self.n - 2) * steady + before[2]

    def unit(self, kind, c):
        return self.base(len(PLAN), UNITS_BEFORE) + self.no[kind, c]

    def split(self, kind, c):
        return self.base(len(PLAN) - TC, SPLITS_BEFORE) + self.split_no[kind, c]

    def bank(self, kind, c):
        return self.banks[kind, c]

    def chunk(self, c):
        return plus(self.n * CH, c)

    def split_by_vector(self, j):
        h, c = divmod(j, TC)
        return plus(self.n * (NH * (TC - 1)), (TC - 1) * h + (c if c >= POOL_CHUNK else c + 1))

    def head(self, h):
        return plus(self.n * NH, h)

    def runs(self, c):
        return c < CH and (c >= 0 or self.follows)


class Before:

    n, first = 0, True
    order = [("y", c) for c in range(FC)] + [("x", c) for c in range(FC)] + [("k", 0), ("q", 0), ("k", 1)]

    def unit(self, kind, c):
        return self.order.index((kind, c))

    split = unit

    def bank(self, kind, c):
        return self.unit(kind, c) % 2


PRE_UNITS = len(Before.order)
FIRST, COLD, LAST = Pass(0, "first"), Pass(1, "cold"), Pass(B, "last")
UNITS_BEFORE = [PRE_UNITS, PRE_UNITS + FIRST.units, PRE_UNITS + FIRST.units + COLD.units]
SPLITS_BEFORE = [PRE_UNITS, PRE_UNITS + FIRST.splits, PRE_UNITS + FIRST.splits + COLD.splits]
END_UNITS = UNITS_BEFORE[2] + len(PLAN) * (B - 2) + LAST.units - EARLY
END_SPLITS = SPLITS_BEFORE[2] + (len(PLAN) - TC) * (B - 2) + LAST.splits - EARLY


def xattn_program(nc, x, ctx, l0wq, l0wk, l0wv, wq, wk, wv, wo, w1, w2, cols, bproj, b2, ident, out):
    x2 = nc.dram_tensor("x2_scratch", (B, T, D), F32, kind="Internal").ap()

    place = [-(-nc.sbuf_base // 64) * 64]

    def sb(name, shape, dt, at=None):
        size = 4 * int(np.prod(shape[1:]))
        if at is None:
            at = place[0]
            place[0] += -(-size // 64) * 64
        return nc.alloc_sbuf_tensor_at(name, shape, dt, offset=at)

    weights_at = place[0]
    wq_s = sb("wq_s", [P, 2, FC, D], F32R)
    wk_s = sb("wk_s", [P, 2, FC, D], F32R)
    wv_s = sb("wv_s", [P, 2, FC, D], F32R)
    wo_s = sb("wo_s", [P, 2, FC, D], F32R)
    w2_at = place[0]
    yT = sb("yT", [P, 2, FC, T], F32R)
    q_hl = sb("q_hl", [P, 2, T], F32R)
    k_hl = sb("k_hl", [P, 2, 2, T], F32R)
    q_st = sb("q_st", [P, G, T], F32R)
    k_st = sb("k_st", [P, G, T], F32R)
    v_s = sb("v_s", [P, TC, NH, VW], F32R)
    oT = sb("oT", [P, 2, FC, T], F32R)
    xT = sb("xT", [P, 2, FC, T], F32R)
    p_hi = sb("p_hi", [P, TC, T], F32R)
    p_lo = sb("p_lo", [P, TC, T], F32R)
    tgt2 = sb("tgt2", [P, TC, D], F32)
    xres = sb("xres", [P, TC, D], F32)
    yt = sb("yt", [P, TC, D], F32)
    xt = sb("xt", [P, TC, D], F32)
    scr_at = place[0]
    o_ab = sb("o_ab", [P, 2, T], F32)
    o_a, o_b = o_ab[:, 0], o_ab[:, 1]
    rs = sb("rs", [P, T], F32)
    rs_t = sb("rs_t", [P, T], F32)
    scr = sb("scr", [P, TC, D], F32, at=scr_at)
    o_raw = sb("o_raw", [P, 2, T], F32)
    bp_s = sb("bp_s", [P, D], F32)
    p_full = sb("p_full", [P, T], F32)
    id_s = sb("id_s", [P, P], F32)
    id_r = sb("id_r", [P, P], F32R)
    col_s = sb("col_s", [P, NCOLS], F32)
    negmax = sb("negmax", [P, 2, TC], F32R)
    rinv = sb("rinv", [P, T // DK], F32)
    stats = sb("stats", [P, TC, 6], F32)
    mv = sb("mv", [P, TC, 2], F32)
    var_e = sb("var_e", [P, TC], F32)
    rstd = sb("rstd", [P, TC], F32)
    m_half = sb("m_half", [P, TC], F32)
    eps_s = sb("eps_s", [P, TC], F32)
    assert place[0] <= nc.sbuf_usable_end, (place[0], nc.sbuf_usable_end)
    w1_hi = sb("w1_hi", [P, FC, FC, D], F32R, at=weights_at)
    w1_lo = sb("w1_lo", [P, FC, FC, D], F32R, at=weights_at + 4 * FC * FC * D)
    w2_hi = sb("w2_hi", [P, HC, D], F32R, at=w2_at)
    w2_lo = sb("w2_lo", [P, HC, D], F32R, at=w2_at + 4 * HC * D)
    b2_s = sb("b2_s", [P, D], F32, at=w2_at + 2 * (4 * HC * D))

    def col(k, c):
        return col_s[:, FC * k + c:FC * k + c + 1]

    GQ, BQ, GKV, BKV, GM, BM = range(6)

    ps_s = nc.alloc_psum_tensor("ps_s", [P, 2, T], F32)
    ps_t = nc.alloc_psum_tensor("ps_t", [P, 2, T], F32)
    ps_o = nc.alloc_psum_tensor("ps_o", [P, T], F32)
    ps_m = nc.alloc_psum_tensor("ps_m", [P, T], F32)
    ps_d = nc.alloc_psum_tensor("ps_d", [P, 2, T], F32)
    turn_banks = [ps_o[:], ps_m[:], ps_d[:, 0], ps_d[:, 1]]
    out_banks = [ps_s[:, 0], ps_s[:, 1], ps_t[:, 0], ps_t[:, 1]]

    sem = nc.alloc_semaphore
    y_loaded = sem("y_loaded")
    x_loaded = sem("x_loaded")
    res_loaded = sem("res_loaded")
    raw_loaded = {k: sem(f"raw_{k}_loaded") for k in ("xt", "xres", "tgt2", "scr")}
    ident_loaded = sem("ident_loaded")
    const_loaded = sem("const_loaded")
    w_hi = sem("w_hi")
    w_split = sem("w_split")
    unit_ready = sem("unit_ready")
    hi_ready = sem("hi_ready")
    split = {k: sem(f"{k}_split") for k in "xyqkvhg"}
    out_done = sem("out_done")
    t2_copied = sem("t2_copied")
    x_summed = sem("x_summed")
    res_summed = sem("res_summed")
    ln_var = sem("ln_var")
    ln_eps = sem("ln_eps")
    ln_rstd = sem("ln_rstd")
    normed = sem("normed")
    stack_loaded = [sem(f"stack_loaded_{j}") for j in range(G)]
    s_ready = sem("s_ready")
    s_maxed = sem("s_maxed")
    m_spread = sem("m_spread")
    m_moved = sem("m_moved")
    t_ready = sem("t_ready")
    p_exp = sem("p_exp")
    p_split = sem("p_split")
    p_pool_split = sem("p_pool_split")
    pv_done = sem("pv_done")
    o_moved = sem("o_moved")
    o_placed = [sem(f"o_placed_{j}") for j in range(G)]
    inv_own = sem("inv_own")
    inv_copied = sem("inv_copied")
    res_own = sem("res_own")
    half_set = sem("half_set")
    inv_ready = sem("inv_ready")
    join_own = sem("join_own")
    o_joined = sem("o_joined")
    consts_set = sem("consts_set")
    ident_set = sem("ident_set")
    stored = sem("stored")
    out_stored = sem("out_stored")
    turned = sem("turned")
    turned_own = sem("turned_own")
    turned_hi = sem("turned_hi")
    y2_done = sem("y2_done")

    def rows(dram, b):
        if isinstance(b, int):
            return dram[b].rearrange("(c p) d -> p c d", p=P)
        return dram[bass.ds(b, 1)].rearrange("a (c p) d -> p (a c) d", p=P)

    pieces = ["l0wk", "l0wq", "l0wv", "wv", "wo", "wk", "wq", "w1_0", "w1_1"]
    pieces += ["w2_0", "w2_1", "w1_2", "w1_3", "w2_2", "w2_3"]
    piece_no = {name: n for n, name in enumerate(pieces)}
    raw_in = {"l0wk": ("tgt2", 1), "l0wv": ("xres", 1), "l0wq": ("scr", 1), "wv": ("xres", 2),
              "wo": ("xres", 3), "wk": ("tgt2", 2), "wq": ("xt", 1), "w1_0": ("xt", 2),
              "w1_1": ("xt", 3), "w2_0": ("tgt2", 3), "w2_1": ("tgt2", 4), "w1_2": ("xt", 4),
              "w1_3": ("scr", 2), "w2_2": ("tgt2", 5), "w2_3": ("xt", 5)}
    raw_buf = {"tgt2": tgt2, "xres": xres, "scr": scr, "xt": xt}
    parts = {"l0wk": wk_s, "l0wv": wv_s, "l0wq": wq_s, "wv": wv_s, "wo": wo_s, "wq": wq_s, "wk": wk_s}
    raw_dram = {"l0wk": l0wk, "l0wv": l0wv, "l0wq": l0wq, "wv": wv, "wo": wo, "wq": wq, "wk": wk}
    for j in range(FC):
        raw_dram[f"w1_{j}"] = w1[j]
        raw_dram[f"w2_{j}"] = w2[:, FC * j:FC * j + FC]

    def hi_of(name):
        if name in parts:
            return parts[name][:, 0]
        j = int(name[-1])
        return w1_hi[:, j] if name[1] == "1" else w2_hi[:, FC * j:FC * j + FC]

    def lo_of(name):
        if name in parts:
            return parts[name][:, 1]
        j = int(name[-1])
        return w1_lo[:, j] if name[1] == "1" else w2_lo[:, FC * j:FC * j + FC]

    block_cm = nc.Block()
    block = block_cm.__enter__()

    @block.sync
    def _(sp):
        def load_raw(name):
            buf, _ = raw_in[name]
            sp.dma_start(raw_buf[buf][:], raw_dram[name]).then_inc(raw_loaded[buf], 16)

        def load_stack(p, h):
            g, j = divmod(h, G)
            q, k = slice(j * DK, j * DK + DK), h % G
            through, projected = p.chunk((h - G) * TC + TC), p.n * G + (g + 1)
            if j == 0 and h >= G and not isinstance(p.n, int):
                through, projected = sp.to_reg(through), sp.to_reg(projected)
            if not (p.first and h < G):
                sp.wait_ge(t_ready, through)
            if j == 0:
                sp.wait_ge(split["q"], projected)
            k_hi = k_hl[q, g % 2, 0].unsqueeze(1).broadcast_to([DK, 2, T])
            for dst, src in ((q_st[0:2 * DK, k], q_hl[q]), (k_st[0:2 * DK, k], k_hi),
                             (q_st[2 * DK:KQ, k], q_hl[q, 0]), (k_st[2 * DK:KQ, k], k_hl[q, g % 2, 1])):
                sp.dma_start(dst.bitcast(F32), src.bitcast(F32)).then_inc(stack_loaded[k], 16)

        def place_head(p, h):
            g, j = divmod(h, G)
            q = slice(j * DK, j * DK + DK)
            moved, joined = p.head(h + 1), plus(p.n * G, g)
            if not isinstance(p.n, int):
                moved, joined = sp.to_reg(moved), sp.to_reg(joined)
            sp.wait_ge(o_moved, moved)
            if not (p.first and g == 0):
                sp.wait_ge(o_joined, joined)
            if p.first and h == 0:
                sp.wait_ge(consts_set, 4)
                sp.wait_ge(w_split, 3)
            sp.dma_start(o_ab[q], o_raw[0:2 * DK, h % 2]).then_inc(o_placed[j], 16)
            sp.dma_start(rs[q.start:q.start + 1], o_raw[2 * DK:2 * DK + 1, h % 2]).then_inc(o_placed[j], 16)

        def attend(p):
            for k in range(p.quarters):
                h = (k - (MOVE_AT + 1)) // TC
                late = 3 if h % G == 0 else 0
                if k % TC == late and p.runs(h * TC):
                    place_head(p, h)
                if (k + STACK_AHEAD) % TC == 0:
                    h = (k + STACK_AHEAD) // TC
                    if h < NH or not (p.first or p.last) and h < NH + 2:
                        load_stack(p, h)
                if p.first:
                    if k == 0:
                        sp.wait_ge(split["x"], FC)
                        load_raw("wq")
                        sp.wait_ge(w_split, 3)
                        load_raw("wv")
                        load_raw("wk")
                    if k == 18:
                        sp.wait_ge(w_split, piece_no["wv"] + 1)
                        load_raw("wo")
                    if k == 60:
                        sp.wait_ge(w_split, piece_no["wq"] + 1)
                        sp.dma_start(xt[:], rows(x, 0)).then_inc(x_loaded, 16)
                    continue
                if k == 1:
                    if not p.last:
                        sp.wait_ge(split["y"], (p.n + 1) * FC)
                        sp.dma_start(yt[:], rows(ctx, p.n)).then_inc(y_loaded, 16)
                        sp.wait_ge(split["x"], (p.n + 1) * FC)
                        sp.dma_start(xt[:], rows(x, p.n)).then_inc(x_loaded, 16)
                    else:
                        sp.wait_ge(split["y"], (B + 1) * FC)
                        sp.wait_ge(stored, 16)
                        sp.dma_start(yt[:], rows(x2, 0)).then_inc(x_loaded, 16)
                        sp.wait_ge(split["x"], (B + 1) * FC)
                        load_raw("w1_0")
                if k == 30:
                    if p.follows:
                        sp.wait_ge(out_done, p.n * TC)
                        sp.dma_start(rows(x2, p.n - 2), xres[:]).then_inc(stored, 16)
                if k == 33:
                    if p.follows:
                        sp.wait_ge(stored, (p.n - 1) * 16)
                    else:
                        sp.wait_ge(out_done, TC)
                    sp.dma_start(xres[:], rows(x, p.n - 1)).then_inc(res_loaded, 16)
                if p.last:
                    if k == 51:
                        sp.wait_ge(split["h"], FC)
                        sp.dma_start(yt[:], rows(x2, 1)).then_inc(x_loaded, 16)
                    if k == 53:
                        sp.wait_ge(w_split, piece_no["w1_0"] + 1)
                        load_raw("w1_1")
                    if k == 61:
                        sp.wait_ge(res_summed, B)
                        load_raw("w2_0")
                    if k == 70:
                        sp.wait_ge(w_split, piece_no["w1_1"] + 1)
                        load_raw("w1_2")

        sp.dma_start(id_s[:], ident).then_inc(ident_loaded, 16)
        sp.dma_start(yt[:], rows(ctx, 0)).then_inc(y_loaded, 16)
        load_raw("l0wk")
        sp.dma_start(xt[:], rows(x, 0)).then_inc(x_loaded, 16)
        load_raw("l0wq")
        load_raw("l0wv")
        sp.dma_start(col_s[:], cols).then_inc(const_loaded, 16)
        sp.dma_start(bp_s[:], bproj.partition_broadcast(P)).then_inc(const_loaded, 16)
        load_stack(FIRST, 0)
        load_stack(FIRST, 1)
        attend(FIRST)
        load_stack(FIRST, NH)
        load_stack(FIRST, NH + 1)
        attend(COLD)
        with sp.Fori(2, B) as i:
            attend(Pass(i))
        attend(LAST)
        sp.wait_ge(w_split, piece_no["w2_0"] + 1)
        load_raw("w2_1")
        sp.wait_ge(o_joined, (B + 1) * G)
        load_raw("w1_3")
        sp.wait_ge(out_done, (B + 1) * TC)
        sp.dma_start(rows(x2, B - 1), xres[:]).then_inc(stored, 16)
        sp.dma_start(b2_s[:], b2.partition_broadcast(P)).then_inc(const_loaded, 16)
        sp.wait_ge(stored, 16 * B)
        sp.dma_start(xres[:], rows(x2, 0)).then_inc(res_loaded, 16)
        for name, before in (("w2_2", "w2_1"), ("w2_3", "w1_2")):
            sp.wait_ge(w_split, piece_no[before] + 1)
            load_raw(name)

        def store_tile(t):
            sp.wait_ge(out_done, t * TC + (B + 2) * TC)
            sp.dma_start(rows(out, t), xres[:]).then_inc(out_stored, 16)

        def load_tile(t, final):
            sp.wait_ge(out_stored, t * 16)
            sp.dma_start(xres[:], rows(x2, t)).then_inc(res_loaded, 16)
            if not final:
                sp.wait_ge(turned, t * FC)
                sp.dma_start(yt[:], rows(x2, t + 1)).then_inc(x_loaded, 16)

        store_tile(0)
        with sp.Fori(1, B - 1) as i:
            load_tile(i, False)
            store_tile(i)
        load_tile(B - 1, True)
        for c in range(TC):
            sp.wait_ge(out_done, 2 * B * TC + (c + 1))
            sp.dma_start(rows(out, B - 1)[:, c], xres[:, c]).then_inc(out_stored, 16)
        sp.wait_ge(out_stored, 16 * (B - 1 + TC))

    @block.tensor
    def _(pe):
        taken = {0: [], 1: []}

        def bank(p, kind, c):
            b = p.bank(kind, c)
            for s, value in taken[b]:
                pe.wait_ge(s, value)
            return ps_d[:, b]

        def filled(ins, p, kind, c, s, value):
            ins.then_inc(unit_ready, 1)
            taken[p.bank(kind, c)] = [(s, value)]

        def transposes(p, kind, c, src, k):
            dst = bank(p, kind, c)
            for t in range(TC):
                ins = nc.tensor.transpose(dst[:, t * P:t * P + P], src[:, t, c * P:c * P + P], id_s[:])
            filled(ins, p, kind, c, split[kind], k + (c + 1))

        def products(dst, lhs, rhs, chunks):
            for c in range(chunks):
                for n, (a, b) in enumerate(((0, 0), (0, 1), (1, 0))):
                    ins = nc.tensor.matmul(dst, lhs(a, c), rhs(b, c), start=(c == 0 and n == 0),
                                           stop=(c == chunks - 1 and n == 2))
            return ins

        def part(p, kind, c, i):
            if kind in "xyh":
                if c == 0:
                    n = {"x": p.n * 2 + 2, "y": p.n * 2 + 1, "h": 2 * B + 1}[kind]
                    pe.wait_ge(normed, n)
                transposes(p, kind, c, xt if kind == "x" else yt, 0 if kind == "h" else (p.n + 1) * FC)
                return
            if kind in "qk":
                w, src, value = (wq_s, xT, p.n * G + (c + 1)) if kind == "q" else (wk_s, yT, p.n * G + (c + 1))
                lhs = [w[:, a, i, (c % G) * P:(c % G) * P + P] for a in range(2)]
                rhs = [src[:, b, i] for b in range(2)]
                if c == G and i == 0:
                    pe.wait_ge(split["x" if kind == "q" else "y"], (p.n + 2) * FC)
                    if p.first:
                        pe.wait_ge(w_split, piece_no["w" + kind] + 1)
            elif kind == "v":
                value = p.n * TC + (c + 1)
                if p.first and c == 0 and i == 0:
                    pe.wait_ge(w_split, 3)
                lhs = [yT[:, a, i, c * P:c * P + P] for a in range(2)]
                rhs = [wv_s[:, b, i] for b in range(2)]
            else:
                n = p.n + 1 if kind == "end" else p.n
                value = (n - 1) * TC + (c + 1)
                lhs = [oT[:, a, i, c * P:c * P + P] for a in range(2)]
                rhs = [wo_s[:, b, i] for b in range(2)]
                if c == 0 and i == 0:
                    pe.wait_ge(o_joined, n * G)
            dst = bank(p, kind, c) if i == 0 else ps_d[:, p.bank(kind, c)]
            for n, (a, b) in enumerate(((0, 0), (0, 1), (1, 0))):
                ins = nc.tensor.matmul(dst, lhs[a], rhs[b], start=(i == 0 and n == 0),
                                       stop=(i == FC - 1 and n == 2))
            if i == FC - 1:
                filled(ins, p, kind, c, out_done if kind in ("out", "end") else split[kind], value)

        def attend(p):
            busy = [(split["q"], p.n * G + 1), (split["k"], p.n * G + 2), (split["x"], (p.n + 1) * FC)]
            taken[0], taken[1] = list(busy), list(busy)
            for k in range(p.quarters):
                if k < CH:
                    h, c = divmod(k, TC)
                    if c == 0:
                        pe.wait_ge(stack_loaded[h % G], (p.n * G + (h // G + 1)) * (16 * STACK_DMAS))
                    if not (p.first and k < 2):
                        pe.wait_ge(s_maxed, p.chunk(k - 1))
                    nc.tensor.matmul(ps_s[:, c % 2], q_st[0:KQ, h % G, c * P:c * P + P],
                                     k_st[0:KQ, h % G], start=True, stop=True).then_inc(s_ready, 1)
                j = k - SHIFT_LAG
                if p.runs(j):
                    h, c = divmod(j, TC)
                    if c == 0:
                        pe.wait_ge(m_moved, p.head(h + 1))
                        if p.first and h == 0:
                            pe.wait_ge(consts_set, 1)
                    if not (p.first and j < 2):
                        if (j - 2) % TC == POOL_CHUNK:
                            pe.wait_ge(p_exp, p.chunk(j - 1))
                        else:
                            pe.wait_ge(p_split, p.split_by_vector(j - 2))
                    nc.tensor.matmul(ps_t[:, c % 2], k_st[0:KM, h % G, c * P:c * P + P],
                                     q_st[0:KM, h % G], start=True, stop=True).then_inc(t_ready, 1)
                for kind, c, i in p.parts.get(k, []):
                    part(p, kind, c, i)
                j = k - WEIGH_LAG
                if p.runs(j):
                    h, c = divmod(j, TC)
                    if c == 0 and not (p.first and h == 0):
                        pe.wait_ge(o_moved, p.head(h))
                    if h == 0:
                        pe.wait_ge(split["v"], p.n * TC + (c + 1))
                        if p.first:
                            pe.wait_ge(consts_set, 2)
                    if c == POOL_CHUNK:
                        pe.wait_ge(p_pool_split, p.head(h + 1))
                    else:
                        pe.wait_ge(p_split, p.split_by_vector(j))
                    for n, src in enumerate((p_hi, p_lo)):
                        ins = nc.tensor.matmul(ps_o[0:VW], v_s[:, c, h % NH], src[:, c],
                                               start=(c == 0 and n == 0), stop=(c == TC - 1 and n == 1))
                    ins.then_inc(pv_done, 1)
                if (k - SPREAD_AT) % TC == 0 and p.runs(k - SPREAD_AT):
                    h = (k - SPREAD_AT) // TC
                    pe.wait_ge(s_maxed, p.chunk(h * TC + TC))
                    if not (p.first and h == 0):
                        pe.wait_ge(m_moved, p.head(h))
                    else:
                        pe.wait_ge(ident_set, 1)
                    for c in range(TC):
                        ins = nc.tensor.matmul(ps_m[0:KM, c * P:c * P + P],
                                               negmax[:, h % 2, c:c + 1].broadcast_to([P, KM]),
                                               id_r[:], start=True, stop=True)
                    ins.then_inc(m_spread, 1)

        pre = Before()
        pe.wait_ge(ident_loaded, 16)
        pe.wait_ge(y_loaded, 16)
        for c in range(FC):
            transposes(pre, "y", c, yt, 0)
        pe.wait_ge(x_loaded, 16)
        for c in range(FC):
            transposes(pre, "x", c, xt, 0)
        pe.wait_ge(split["y"], FC)
        pe.wait_ge(w_split, 1)
        for i in range(FC):
            part(pre, "k", 0, i)
        pe.wait_ge(split["x"], FC)
        pe.wait_ge(w_split, 2)
        for i in range(FC):
            part(pre, "q", 0, i)
        for i in range(FC):
            part(pre, "k", 1, i)

        attend(FIRST)
        for c in range(TC):
            dst = bank(FIRST, "next v", c)
            ins = products(dst, lambda a, i: yT[:, a, i, c * P:c * P + P], lambda b, i: wv_s[:, b, i], FC)
            filled(ins, FIRST, "next v", c, split["v"], TC + c + 1)
        pe.wait_ge(o_joined, G)
        for t in range(TC):
            dst = bank(FIRST, "out", t)
            for c in range(FC):
                ins = nc.tensor.transpose(dst[:, c * P:c * P + P], xres[:, c, t * P:t * P + P], id_s[:])
            filled(ins, FIRST, "out", t, out_done, t + 1)
        pe.wait_ge(normed, 2)
        for c in range(FC):
            transposes(FIRST, "x", c, xt, FC)
        for i in range(FC):
            part(FIRST, "q", G, i)
        attend(COLD)
        with pe.Fori(2, B) as i:
            attend(Pass(i))
        attend(LAST)

        def hidden(t, c):
            first_tile = isinstance(t, int) and t == 0
            if c >= 2:
                pe.wait_ge(split["g"], t * HC + (c - 1))
            if first_tile and c == EARLY:
                pe.wait_ge(out_done, (B + 1) * TC)
            if first_tile and c % FC == 0:
                pe.wait_ge(w_split, piece_no[f"w1_{c // FC}"] + 1)
            q, j = divmod(c, FC)
            w = (w1_hi, w1_lo)
            for k in range(FC):
                if c < 2 and k in (0, FC - 1):
                    pe.wait_ge(split["h"], t * FC + (FC - 1 if c == 0 and k == 0 and not first_tile else FC))
                for n, (a, b) in enumerate(((0, 0), (0, 1), (1, 0))):
                    ins = nc.tensor.matmul(ps_d[:, c % 2], w[a][:, q, k, j * P:j * P + P], xT[:, b, k],
                                           start=(k == 0 and n == 0), stop=(k == FC - 1 and n == 2))
            ins.then_inc(unit_ready, 1)

        def output(t, c):
            if c == 0 and not (isinstance(t, int) and t == 0):
                pe.wait_ge(out_done, (t + (B + 1)) * TC)
            if isinstance(t, int) and t == 0 and c % FC == 0:
                pe.wait_ge(w_split, piece_no[f"w2_{c // FC}"] + 1)
            pe.wait_ge(split["g"], t * HC + (c + 1))
            g, w = (p_hi, p_lo), (w2_hi, w2_lo)
            for k in range(TC):
                for n, (a, b) in enumerate(((0, 0), (0, 1), (1, 0))):
                    ins = nc.tensor.matmul(out_banks[k], g[a][:, c % TC, k * P:k * P + P], w[b][:, c],
                                           start=(c == 0 and n == 0), stop=(c == HC - 1 and n == 2))
                ins.then_inc(y2_done, 1)

        def turn(t, k):
            if k == 0:
                pe.wait_ge(normed, t + (2 * B + 2))
            elif k >= 2:
                pe.wait_ge(split["g"], t * HC + (HC - 3 + k))
            for r in range(TC):
                ins = nc.tensor.transpose(turn_banks[k][:, r * P:r * P + P], yt[:, r, k * P:k * P + P], id_s[:])
            ins.then_inc(turned, 1)

        def tile(t, final, early):
            for c in range(early, HC):
                hidden(t, c)
                if c == TURN_AT and not final:
                    turn(t, 0)
                    turn(t, 1)
                if c == HC - 1 and not final:
                    turn(t, 2)
                if c >= 1:
                    output(t, c - 1)
            if not final:
                turn(t, 3)
            output(t, HC - 1)

        for c in range(EARLY):
            hidden(0, c)
        taken[0], taken[1] = [(split["g"], EARLY - 1)], [(split["g"], EARLY)]
        for c in range(TC):
            for i in range(FC):
                part(LAST, "end", c, i)
        for c in range(EARLY - 1):
            output(0, c)
        tile(0, False, EARLY)
        with pe.Fori(1, B - 1) as i:
            tile(i, False, 0)
        tile(B - 1, True, 0)

    @block.scalar
    def _(act):
        def hi_weights(name):
            buf, use = raw_in[name]
            act.wait_ge(raw_loaded[buf], 16 * use)
            act.activation(hi_of(name), raw_buf[buf][:], ACT.Identity).then_inc(w_hi, 1)

        def hi_plain(p, kind, c, dst, src):
            act.wait_ge(unit_ready, p.unit(kind, c) + 1)
            act.activation(dst, src, ACT.Identity).then_inc(hi_ready, 1)

        def hi_affine(p, kind, c, dst, gain, bias):
            act.wait_ge(unit_ready, p.unit(kind, c) + 1)
            b = ps_d[:, p.bank(kind, c)]
            act.activation(dst, b, ACT.Identity, bias=col(bias, c), scale=col(gain, c))
            act.activation(b, b, ACT.Identity, bias=col(bias, c), scale=col(gain, c)).then_inc(hi_ready, 1)

        def hi(p, kind, c):
            if kind in "xyh":
                gain, bias = {"x": (GQ, BQ), "y": (GKV, BKV), "h": (GM, BM)}[kind]
                hi_affine(p, kind, c, (yT if kind == "y" else xT)[:, 0, c], gain, bias)
            elif kind == "v":
                if p.follows:
                    act.wait_ge(pv_done, p.chunk(c + 1 - TC))
                hi_value(p, "v", c)
            else:
                groups = p.n * G + (c if kind == "q" else c - 1)
                if not (p.first and c <= (0 if kind == "q" else 1)):
                    for j in range(G):
                        act.wait_ge(stack_loaded[j], groups * (16 * STACK_DMAS))
                dst = q_hl[:, 0] if kind == "q" else k_hl[:, c % 2, 0]
                hi_plain(p, kind, c, dst, ps_d[:, p.bank(kind, c)])

        def hi_value(p, kind, c):
            hi_plain(p, kind, c, v_s[:, c, :, 0:2 * DK:2],
                     ps_d[:, p.bank(kind, c)].rearrange("p (h d) -> p h d", h=NH))

        def attend(p):
            for k in range(p.quarters):
                if (k - MAXIMA_AT) % TC == 0 and p.runs(k - MAXIMA_AT):
                    h = (k - MAXIMA_AT) // TC
                    act.wait_ge(m_spread, p.head(h + 1))
                    act.activation(q_st[KQ:KM, h % G], ps_m[KQ:KM], ACT.Identity).then_inc(m_moved, 1)
                j = k - SHIFT_LAG
                if p.runs(j):
                    c = j % TC
                    act.wait_ge(t_ready, p.chunk(j + 1))
                    if not (p.first and j < TC):
                        act.wait_ge(pv_done, p.chunk(j + 1 - TC))
                    act.activation(p_hi[:, c], ps_t[:, c % 2], ACT.Exp, scale=SCALE)
                    whole = ps_t[:, c % 2]
                    if c == POOL_CHUNK:
                        whole = p_full[:]
                        if not (p.first and j < TC):
                            act.wait_ge(p_pool_split, p.head(j // TC))
                    act.activation(whole, ps_t[:, c % 2], ACT.Exp, scale=SCALE).then_inc(p_exp, 1)
                if (k - MOVE_AT) % TC == 0 and p.runs(k - MOVE_AT):
                    h = (k - MOVE_AT) // TC
                    act.wait_ge(pv_done, p.chunk(h * TC + TC))
                    if not (p.first and h < 2):
                        placed = plus(p.n * G, (h - 2) // G + 1)
                        act.wait_ge(o_placed[(h - 2) % G], placed * (16 * PLACE_DMAS))
                    act.activation(o_raw[0:VW, h % 2], ps_o[0:VW], ACT.Identity).then_inc(o_moved, 1)
                for kind, c in p.his.get(k, []):
                    hi(p, kind, c)
                if p.first:
                    if k == 12:
                        act.wait_ge(unit_ready, p.unit("v", TC - 1) + 1)
                        hi_weights("wv")
                    if k == 22:
                        hi_weights("wo")
                    if k == 32:
                        act.wait_ge(unit_ready, p.unit("k", 3) + 1)
                        hi_weights("wk")
                    if k == 40:
                        act.wait_ge(unit_ready, p.unit("q", 3) + 1)
                        hi_weights("wq")
                if p.last:
                    if k == 42:
                        hi_weights("w1_0")
                    if k == 57:
                        hi_weights("w1_1")
                    if k == 66:
                        hi_weights("w2_0")

        pre = Before()
        act.wait_ge(ident_loaded, 16)
        act.activation(id_r[:], id_s[:], ACT.Identity).then_inc(ident_set, 1)
        for c in range(FC):
            hi_plain(pre, "y", c, yT[:, 0, c], ps_d[:, pre.bank("y", c)])
        hi_weights("l0wk")
        for c in range(FC):
            hi_plain(pre, "x", c, xT[:, 0, c], ps_d[:, pre.bank("x", c)])
        hi_weights("l0wq")
        hi(pre, "k", 0)
        hi_weights("l0wv")
        hi(pre, "q", 0)
        hi(pre, "k", 1)
        act.wait_ge(const_loaded, 32)
        attend(FIRST)
        for c in range(TC):
            hi_value(FIRST, "next v", c)
        act.wait_ge(w_split, piece_no["wk"] + 1)
        for t in range(TC):
            act.wait_ge(unit_ready, FIRST.unit("out", t) + 1)
            act.activation(tgt2[:, t], ps_d[:, FIRST.bank("out", t)], ACT.Identity).then_inc(t2_copied, 1)
        for c in range(FC):
            hi(FIRST, "x", c)
        hi(FIRST, "q", G)
        attend(COLD)
        with act.Fori(2, B) as i:
            attend(Pass(i))
        attend(LAST)

        def gelu(t, c, unit):
            act.wait_ge(unit_ready, unit + 1)
            if not (isinstance(t, int) and t == 0 and c < TC):
                act.wait_ge(y2_done, t * (HC * TC) + (c - TC + 1) * TC)
            elif c == 0:
                act.wait_ge(pv_done, (B + 1) * CH)
            b1 = col_s[:, 6 * FC + c:6 * FC + c + 1]
            act.activation(p_hi[:, c % TC], ps_d[:, c % 2], ACT.Gelu, bias=b1)
            act.activation(ps_d[:, c % 2], ps_d[:, c % 2], ACT.Gelu, bias=b1).then_inc(hi_ready, 1)

        def gain_and_bias(dst, k):
            return act.activation(dst, turn_banks[k], ACT.Identity, bias=col(BM, k), scale=col(GM, k))

        def tile(t, final, early):
            for c in range(early, HC):
                if isinstance(t, int) and t == 0 and c in (4, 6, 8):
                    hi_weights({4: "w1_3", 6: "w2_2", 8: "w2_3"}[c])
                gelu(t, c, t * HC + (END_UNITS + c))
                if c == TURN_AT + 1 and not final:
                    for k in range(2):
                        act.wait_ge(turned, t * FC + (k + 1))
                        gain_and_bias(turn_banks[k], k).then_inc(turned_own, 1)
            if not final:
                for k in range(FC):
                    if k < 2:
                        act.wait_ge(turned_own, t * 2 + (k + 1))
                        act.activation(xT[:, 0, k], turn_banks[k], ACT.Identity).then_inc(turned_hi, 1)
                    else:
                        act.wait_ge(turned, t * FC + (k + 1))
                        gain_and_bias(xT[:, 0, k], k)
                        gain_and_bias(turn_banks[k], k).then_inc(turned_hi, 1)

        for c in range(EARLY):
            gelu(0, c, LAST.unit("g", c))
            if c == 1:
                hi_weights("w2_1")
        hi_weights("w1_2")
        tile(0, False, EARLY)
        with act.Fori(1, B - 1) as i:
            tile(i, False, 0)
        tile(B - 1, True, 0)

    @block.vector
    def _(dve):
        def lo(p, kind, c, dst, src, hi):
            dve.wait_ge(hi_ready, p.split(kind, c) + 1)
            dve.tensor_tensor(dst, src, hi, ALU.subtract).then_inc(split[kind[-1]], 1)

        def lo_unit(p, kind, c):
            b = ps_d[:, p.bank(kind, c)]
            if kind in "xyh":
                dst = yT if kind == "y" else xT
                lo(p, kind, c, dst[:, 1, c], b, dst[:, 0, c].bitcast(F32))
            elif kind in ("v", "next v"):
                lo(p, kind, c, v_s[:, c, :, 1:2 * DK:2], b.rearrange("p (h d) -> p h d", h=NH),
                   v_s[:, c, :, 0:2 * DK:2].bitcast(F32))
            elif kind == "q":
                lo(p, kind, c, q_hl[:, 1], b, q_hl[:, 0].bitcast(F32))
            else:
                lo(p, kind, c, k_hl[:, c % 2, 1], b, k_hl[:, c % 2, 0].bitcast(F32))

        def norm_stats(rows_in):
            for t in range(TC):
                dve.bn_stats(stats[:, t], rows_in[:, t])
            norm_aggregate()

        def norm_aggregate():
            dve.drain()
            for t in range(TC):
                ins = dve.bn_aggr(mv[:, t], stats[:, t])
            ins.then_inc(ln_var, 1)

        def norm_apply(rows_in, t, n):
            if t == 0:
                dve.wait_ge(ln_rstd, n + 1)
            ins = dve.tensor_scalar(rows_in[:, t], rows_in[:, t], mv[:, t, 0:1], rstd[:, t:t + 1],
                                    ALU.subtract, ALU.mult)
            if t == TC - 1:
                ins.then_inc(normed, 1)

        def invert(p, g, step):
            done = plus(p.n * G, g)
            if step == 0:
                for j in range(G):
                    dve.wait_ge(o_placed[j], (done + 1) * (16 * PLACE_DMAS))
                dve.transpose(rs_t[:], rs[:]).then_inc(inv_own, 1)
            elif step == 1:
                dve.wait_ge(inv_own, done * 2 + 1)
                sums = rs_t[:].rearrange("p (b e) -> p b e", e=DK)[:, :, 0]
                dve.reciprocal(rinv[:], sums).then_inc(inv_own, 1)
            elif step == 2:
                dve.wait_ge(inv_own, done * 2 + 2)
                dve.tensor_copy(rs_t[:].rearrange("p (b e) -> p b e", e=DK),
                                rinv[:].unsqueeze(2).broadcast_to([P, T // DK, DK])).then_inc(inv_copied, 1)
            else:
                dve.wait_ge(inv_copied, done + 1)
                dve.transpose(rs[:], rs_t[:]).then_inc(inv_ready, 1)

        def residual(p, kind, t):
            if t == 0:
                dve.wait_ge(res_summed, B if kind == "end" else p.n - 1)
            dve.wait_ge(unit_ready, p.unit(kind, t) + 1)
            dve.tensor_tensor(xres[:, t], ps_d[:, p.bank(kind, t)], xres[:, t], ALU.add)\
               .then_inc(out_done, 1)

        def attend(p):
            for k in range(p.quarters):
                if p.runs(k - 1):
                    h, c = divmod(k - 1, TC)
                    dve.wait_ge(s_ready, p.chunk(k))
                    if c == 0 and not (p.first and h < 2):
                        dve.wait_ge(m_spread, p.head(h - 1))
                    dve.tensor_reduce(negmax[:, h % 2, c:c + 1], ps_s[:, c % 2], AX.X, ALU.max,
                                      negate=True).then_inc(s_maxed, 1)
                j = k - (SHIFT_LAG + 1)
                if p.runs(j) and j % TC != POOL_CHUNK:
                    c = j % TC
                    dve.wait_ge(p_exp, p.chunk(j + 1))
                    dve.tensor_tensor(p_lo[:, c], ps_t[:, c % 2], p_hi[:, c].bitcast(F32),
                                      ALU.subtract).then_inc(p_split, 1)
                for kind, c in p.los.get(k, []):
                    if kind == "out":
                        residual(p, kind, c)
                    else:
                        lo_unit(p, kind, c)
                g, step = divmod(k - INVERT_AT, TC * G)
                if step < 4 and p.runs(g * TC * G) and not (g == G - 1 and p.quarters > CH):
                    invert(p, g, step)
                if 4 <= k < 8:
                    if k == 4 and p.last:
                        dve.wait_ge(x_loaded, (B + 2) * 16)
                    elif k == 4 and not p.first:
                        dve.wait_ge(y_loaded, (p.n + 1) * 16)
                    dve.bn_stats(stats[:, k - 4], yt[:, k - 4])
                if k == 8:
                    norm_aggregate()
                if 12 <= k < 16:
                    norm_apply(yt, k - 12, p.n * 2)
                if not (p.first or p.last):
                    if 18 <= k < 22:
                        dve.wait_ge(x_summed, p.n * TC + (k - 17))
                        dve.bn_stats(stats[:, k - 18], xt[:, k - 18])
                    if k == 22:
                        norm_aggregate()
                    if 25 <= k < 29:
                        norm_apply(xt, k - 25, p.n * 2 + 1)

        dve.memset(k_st[KQ:KM].bitcast(F32), 1.0).then_inc(consts_set, 1)
        dve.memset(v_s[:, :, :, 2 * DK:VW].bitcast(F32), 1.0).then_inc(consts_set, 1)
        pre = Before()
        for kind, c in pre.order:
            lo_unit(pre, kind, c)
        dve.wait_ge(w_split, 2)
        dve.memset(rs[:], 1.0).then_inc(consts_set, 1)
        dve.memset(rs_t[:], 1.0).then_inc(consts_set, 1)
        attend(FIRST)
        for c in range(TC):
            lo_unit(FIRST, "next v", c)
        for step in range(4):
            invert(FIRST, G - 1, step)
        dve.wait_ge(x_loaded, 32)
        for t in range(TC):
            dve.wait_ge(t2_copied, t + 1)
            dve.tensor_tensor(xt[:, t], ps_d[:, FIRST.bank("out", t)], xt[:, t], ALU.add).then_inc(x_summed, 1)
            dve.wait_ge(x_summed, t + 1)
            dve.sem_inc(out_done, 1)
            dve.bn_stats(stats[:, t], xt[:, t])
        norm_aggregate()
        for t in range(TC):
            norm_apply(xt, t, 1)
        for c in range(FC):
            lo_unit(FIRST, "x", c)
        lo_unit(FIRST, "q", G)
        attend(COLD)
        with dve.Fori(2, B) as i:
            attend(Pass(i))
        attend(LAST)

        def lo_hidden(t, c):
            dve.wait_ge(hi_ready, t * HC + (END_SPLITS + c + 1))
            dve.tensor_tensor(p_lo[:, c % TC], ps_d[:, c % 2], p_hi[:, c % TC].bitcast(F32),
                              ALU.subtract).then_inc(split["g"], 1)

        def tile(t, final, early):
            for c in range(early, HC):
                lo_hidden(t, c)
                if c == 7 and not final:
                    dve.wait_ge(x_loaded, (t + (B + 3)) * 16)
                    norm_stats(yt)
                if c == 9 and not final:
                    for r in range(TC):
                        norm_apply(yt, r, t + (2 * B + 1))
            if not final:
                for k in range(FC):
                    dve.wait_ge(turned_hi, t * FC + (k + 1))
                    dve.tensor_tensor(xT[:, 1, k], turn_banks[k], xT[:, 0, k].bitcast(F32),
                                      ALU.subtract).then_inc(split["h"], 1)
            dve.wait_ge(res_summed, t + (B + 1))
            for k in range(TC):
                dve.wait_ge(y2_done, t * (HC * TC) + ((HC - 1) * TC + k + 1))
                dve.tensor_tensor(xres[:, k], out_banks[k], xres[:, k], ALU.add).then_inc(out_done, 1)

        lo_hidden(0, 0)
        for step in range(4):
            invert(LAST, G - 1, step)
        for c in range(1, EARLY):
            lo_hidden(0, c)
        for t in range(TC):
            residual(LAST, "end", t)
        tile(0, False, EARLY)
        with dve.Fori(1, B - 1) as i:
            tile(i, False, 0)
        tile(B - 1, True, 0)

    @block.gpsimd
    def _(pool):
        def lo_weights(name, c):
            buf, _ = raw_in[name]
            if c == 0:
                pool.wait_ge(w_hi, piece_no[name] + 1)
            ins = pool.tensor_tensor(lo_of(name)[:, c], raw_buf[buf][:, c], hi_of(name)[:, c].bitcast(F32),
                                     ALU.subtract)
            if c == FC - 1:
                ins.then_inc(w_split, 1)

        def norm_rstd(n):
            pool.wait_ge(ln_var, n + 1)
            pool.tensor_tensor(var_e[:], mv[:, :, 1], eps_s[:], ALU.add).then_inc(ln_eps, 1)
            pool.wait_ge(ln_eps, n + 1)
            pool.tensor_tensor(rstd[:], var_e[:], m_half[:], ALU.pow).then_inc(ln_rstd, 1)

        def join(p, g, step):
            done = plus(p.n * G, g)
            if step == 0:
                for j in range(G):
                    pool.wait_ge(o_placed[j], (done + 1) * (16 * PLACE_DMAS))
                pool.tensor_tensor(o_a, o_a, o_b, ALU.add).then_inc(join_own, 1)
            elif step == 1:
                pool.wait_ge(join_own, done * 3 + 1)
                pool.wait_ge(inv_ready, done + 1)
                if p.first:
                    if g == 0:
                        pool.wait_ge(w_split, piece_no["wo"] + 1)
                    pool.tensor_tensor(xres[:, g], o_a, rs[:], ALU.mult).then_inc(o_joined, 1)
                    pool.sem_inc(join_own, 2)
                    return
                if g == 0 and p.follows:
                    pool.wait_ge(unit_ready, p.unit("out", TC - 1) + 1)
                pool.tensor_tensor(oT[:, 0, g % G], o_a, rs[:], ALU.mult).then_inc(join_own, 1)
            elif step == 2 and not p.first:
                pool.tensor_tensor(o_a, o_a, rs[:], ALU.mult).then_inc(join_own, 1)
            elif step == 3 and not p.first:
                pool.wait_ge(join_own, done * 3 + 3)
                pool.tensor_tensor(oT[:, 1, g % G], o_a, oT[:, 0, g % G].bitcast(F32), ALU.subtract)\
                    .then_inc(o_joined, 1)

        def sum_x(p, t):
            if t == 0:
                pool.wait_ge(x_loaded, (p.n + 2) * 16)
                if p.cold:
                    pool.wait_ge(t2_copied, TC)
            pool.tensor_tensor(xt[:, t], xt[:, t], tgt2[:, t], ALU.add).then_inc(x_summed, 1)

        def sum_res(p, t, bias):
            if not bias:
                if t == 0:
                    pool.wait_ge(res_loaded, p.n * 16)
                pool.tensor_tensor(xres[:, t], xres[:, t], tgt2[:, t], ALU.add).then_inc(res_own, 1)
                return
            pool.wait_ge(res_own, p.n * TC - (TC - t - 1))
            ins = pool.tensor_tensor(xres[:, t], xres[:, t], bp_s[:], ALU.add)
            if t == TC - 1:
                ins.then_inc(res_summed, 1)

        def attend(p):
            sum_x_at, sum_res_at, bias_at = (5, 6, 7, 9), (49, 50, 51, 53), (54, 55, 57, 59)
            weights_at = {}
            if p.first:
                weights_at = {13: "wv", 22: "wo", 33: "wk", 44: "wq"}
            if p.last:
                weights_at = {43: "w1_0", 64: "w1_1", 71: "w2_0"}
            for k in range(p.quarters):
                j = k - (SHIFT_LAG + 1)
                if p.runs(j) and j % TC == POOL_CHUNK:
                    pool.wait_ge(p_exp, p.chunk(j + 1))
                    pool.tensor_tensor(p_lo[:, POOL_CHUNK], p_full[:], p_hi[:, POOL_CHUNK].bitcast(F32),
                                       ALU.subtract).then_inc(p_pool_split, 1)
                if not p.first and not p.last:
                    if k in sum_x_at:
                        sum_x(p, sum_x_at.index(k))
                    if k == 23:
                        norm_rstd(p.n * 2 + 1)
                if k == 11:
                    norm_rstd(p.n * 2)
                if not p.first:
                    if k in sum_res_at:
                        sum_res(p, sum_res_at.index(k), False)
                    if k in bias_at:
                        sum_res(p, bias_at.index(k), True)
                g, at = divmod(k - INVERT_AT, TC * G)
                steps = (0, 5, 6, 7) if g == 0 else (0, 3, 4, 5)
                if at in steps and p.runs(g * TC * G) and not (p.first and g == G - 1):
                    join(p, g, steps.index(at))
                for at, name in weights_at.items():
                    if k == at and name == "w2_0":
                        pool.wait_ge(t_ready, (B + 1) * CH)
                    if at <= k < at + FC:
                        lo_weights(name, k - at)

        pool.memset(m_half[:], -0.5).then_inc(half_set, 1)
        pool.memset(eps_s[:], EPS).then_inc(half_set, 1)
        pool.wait_ge(half_set, 2)
        for name in ("l0wk", "l0wq", "l0wv"):
            for c in range(FC):
                lo_weights(name, c)
        attend(FIRST)
        join(FIRST, G - 1, 0)
        join(FIRST, G - 1, 1)
        norm_rstd(1)
        attend(COLD)
        with pool.Fori(2, B) as i:
            attend(Pass(i))
        attend(LAST)

        def add_bias(t):
            pool.wait_ge(res_loaded, (t + (B + 1)) * 16)
            if isinstance(t, int) and t == 0:
                pool.wait_ge(const_loaded, 48)
            pool.tensor_tensor(xres[:], xres[:], b2_s[:].unsqueeze(1).broadcast_to([P, TC, D]),
                               ALU.add).then_inc(res_summed, 1)

        for name in ("w2_1", "w1_2"):
            if name == "w1_2":
                pool.wait_ge(out_done, (B + 1) * TC)
            for c in range(FC):
                lo_weights(name, c)
        add_bias(0)
        for name in ("w1_3", "w2_2", "w2_3"):
            for c in range(FC):
                lo_weights(name, c)
        norm_rstd(2 * B + 1)
        with pool.Fori(1, B - 1) as i:
            add_bias(i)
            norm_rstd(i + (2 * B + 1))
        add_bias(B - 1)

    block_cm.__exit__(None, None, None)


def kernel(x, ctx_1024, L0_xattn_Wq, L0_xattn_Wk, L0_xattn_Wv, L1_xattn_gq, L1_xattn_bq, L1_xattn_gkv,
           L1_xattn_bkv, L1_xattn_Wq, L1_xattn_Wkv, L1_xattn_Wproj, L1_xattn_bproj, L1_xattn_gm,
           L1_xattn_bm, L1_xattn_W1, L1_xattn_b1, L1_xattn_W2, L1_xattn_b2):
    import concourse.bacc as bacc
    from concourse.bass_utils import run_bass_kernel_spmd

    def chunked(w):
        w = np.asarray(w)
        return np.ascontiguousarray(w.reshape(-1, P, w.shape[1]).transpose(1, 0, 2))

    def columns(v):
        return np.asarray(v).reshape(-1, P).T

    wkv = np.asarray(L1_xattn_Wkv)
    w1 = np.asarray(L1_xattn_W1).reshape(FC, P, FC, D).transpose(2, 1, 0, 3)
    arrays = {
        "x": np.ascontiguousarray(x),
        "ctx": np.ascontiguousarray(ctx_1024),
        "l0wq": chunked(np.asarray(L0_xattn_Wq).T),
        "l0wk": chunked(np.asarray(L0_xattn_Wk).T),
        "l0wv": chunked(np.asarray(L0_xattn_Wv).T),
        "wq": chunked(L1_xattn_Wq),
        "wk": chunked(wkv[:, :D]),
        "wv": chunked(wkv[:, D:]),
        "wo": chunked(L1_xattn_Wproj),
        "w1": np.ascontiguousarray(w1),
        "w2": chunked(L1_xattn_W2),
        "cols": np.ascontiguousarray(np.concatenate(
            [columns(v) for v in (L1_xattn_gq, L1_xattn_bq, L1_xattn_gkv, L1_xattn_bkv, L1_xattn_gm,
                                  L1_xattn_bm, L1_xattn_b1)], axis=1)),
        "bproj": np.ascontiguousarray(L1_xattn_bproj),
        "b2": np.ascontiguousarray(L1_xattn_b2),
        "ident": np.eye(P, dtype=np.float32),
    }
    nc = bacc.Bacc("TRN2", target_bir_lowering=False, num_devices=1, dynamic_dma_scratch_size=1024)
    args = [nc.dram_tensor(name, a.shape, mybir.dt.from_np(a.dtype), kind="ExternalInput").ap()
            for name, a in arrays.items()]
    out = nc.dram_tensor("out", (B, T, D), F32, kind="ExternalOutput").ap()
    xattn_program(nc, *args, out)
    r = run_bass_kernel_spmd(nc, [arrays], core_ids=[0])
    return r.results[0]["out"]
```
